# Optimizing a Trainium2 kernel written in Bass

```python
import numpy as np
import jax
import jax.numpy as jnp

def _softmax(x, axis=-1):
    return jax.nn.softmax(x, axis=axis)

def _gelu(x):
    return jax.nn.gelu(x, approximate=True)

def _silu(x):
    return jax.nn.silu(x)

def _sigmoid(x):
    return jax.nn.sigmoid(x)

def _layernorm(x, axis=-1, eps=1e-05):
    m = jnp.mean(x, axis=axis, keepdims=True)
    v = jnp.var(x, axis=axis, keepdims=True)
    return (x - m) / jnp.sqrt(v + eps)

def _scatter_add(tgt, idx, src, axis=0):
    return tgt.at[idx].add(src)

def _segment_sum(src, seg, n):
    return jax.ops.segment_sum(src, seg, n)
kernel_name = 'mk_gnn_preln_d2_gnn_r8_aed7eb'

def setup_inputs(seed: int=0):
    np.random.seed(seed)
    _w = jnp.asarray

    def _rec_inputs():
        import jax
        import jax.numpy as jnp
        _gk = jax.random.key(seed)
        x = -0.0002117 + 1 * jax.random.normal(jax.random.fold_in(_gk, 1), (6250, 256), jnp.float32)
        src = jax.random.randint(jax.random.fold_in(_gk, 2), (100000,), 0, 6250, jnp.int32)
        dst = jnp.minimum((6250 * jax.random.uniform(jax.random.fold_in(_gk, 3), (100000,)) ** 2.0).astype(jnp.int32), 49999)
        _o = jnp.argsort(dst, stable=True)
        src = src[_o]
        dst = dst[_o]
        return (x, src, dst)
    x, src, dst = _rec_inputs()

    def _L0_gnn_setup():
        import jax, jax.numpy as jnp
        import numpy as np
        N_NODES = 12500
        N_EDGES = 37500
        DIM = 256
        LN_EPS = 1e-05
        key = jax.random.key(seed)
        ks = jax.random.split(key, 4)
        scale = 1.0 / np.sqrt(DIM)
        h = jax.random.normal(ks[0], (N_NODES, DIM), dtype=jnp.float32)
        edge_index = jax.random.randint(ks[1], (2, N_EDGES), 0, N_NODES, dtype=jnp.int64)
        W1 = jax.random.normal(ks[2], (DIM, DIM), dtype=jnp.float32) * scale
        b1 = jnp.zeros((DIM,), dtype=jnp.float32)
        W2 = jax.random.normal(ks[3], (DIM, DIM), dtype=jnp.float32) * scale
        b2 = jnp.zeros((DIM,), dtype=jnp.float32)
        eps = jnp.zeros((), dtype=jnp.float32)
        gamma = jnp.ones((DIM,), dtype=jnp.float32)
        beta = jnp.zeros((DIM,), dtype=jnp.float32)
        return {'h': h, 'edge_index': edge_index, 'W1': W1, 'b1': b1, 'W2': W2, 'b2': b2, 'eps': eps, 'gamma': gamma, 'beta': beta}
    _L0_gnn_all = _L0_gnn_setup()
    _L0_gnn_in = {k: v for k, v in _L0_gnn_all.items() if k in ('W1', 'b1', 'W2', 'b2', 'eps', 'gamma', 'beta')}
    del _L0_gnn_all

    def _L1_gnn_setup():
        import jax, jax.numpy as jnp
        import numpy as np
        N = 2500
        E = 40000
        HID = 256
        H = 4
        D = HID // H
        FF = 4 * HID

        def _layernorm(x, g, b, eps=1e-05):
            mu = jnp.mean(x, axis=-1, keepdims=True)
            var = jnp.var(x, axis=-1, keepdims=True)
            return (x - mu) * jax.lax.rsqrt(var + eps) * g + b

        def _transformer_conv(x, edge_index, Wq, bq, Wk, bk, Wv, bv, Wskip, bskip):
            src, dst = (edge_index[0], edge_index[1])
            n = x.shape[0]
            q = (x @ Wq + bq).reshape(n, H, D)
            k = (x @ Wk + bk).reshape(n, H, D)
            v = (x @ Wv + bv).reshape(n, H, D)
            qi = q[dst]
            kj = k[src]
            vj = v[src]
            alpha = jnp.sum(qi * kj, axis=-1) / jnp.sqrt(jnp.float32(D))
            m = jax.ops.segment_max(alpha, dst, num_segments=n)
            ex = jnp.exp(alpha - m[dst])
            denom = jax.ops.segment_sum(ex, dst, num_segments=n)
            a = ex / (denom[dst] + 1e-16)
            out = jax.ops.segment_sum(a[..., None] * vj, dst, num_segments=n)
            out = out.reshape(n, H * D)
            return out + x @ Wskip + bskip
        key = jax.random.key(seed)
        ks = jax.random.split(key, 20)
        w = lambda i, sh: jax.random.normal(ks[i], sh, dtype=jnp.float32) * 0.02
        return {'x': jax.random.normal(ks[0], (N, HID), dtype=jnp.float32), 'edge_index': jax.random.randint(ks[1], (2, E), 0, N, dtype=jnp.int64), 'Wq': w(2, (HID, HID)), 'bq': jnp.zeros((HID,), jnp.float32), 'Wk': w(3, (HID, HID)), 'bk': jnp.zeros((HID,), jnp.float32), 'Wv': w(4, (HID, HID)), 'bv': jnp.zeros((HID,), jnp.float32), 'Wskip': w(5, (HID, HID)), 'bskip': jnp.zeros((HID,), jnp.float32), 'ln1_g': jnp.ones((HID,), jnp.float32), 'ln1_b': jnp.zeros((HID,), jnp.float32), 'W1': w(6, (HID, FF)), 'b1': jnp.zeros((FF,), jnp.float32), 'W2': w(7, (FF, HID)), 'b2': jnp.zeros((HID,), jnp.float32), 'ln2_g': jnp.ones((HID,), jnp.float32), 'ln2_b': jnp.zeros((HID,), jnp.float32)}
    _L1_gnn_all = _L1_gnn_setup()
    _L1_gnn_in = {k: v for k, v in _L1_gnn_all.items() if k in ('Wq', 'bq', 'Wk', 'bk', 'Wv', 'bv', 'Wskip', 'bskip', 'ln1_g', 'ln1_b', 'W1', 'b1', 'W2', 'b2', 'ln2_g', 'ln2_b')}
    del _L1_gnn_all
    return {'x': x, 'src': src, 'dst': dst, 'L0_gnn_W1': _L0_gnn_in['W1'], 'L0_gnn_b1': _L0_gnn_in['b1'], 'L0_gnn_W2': _L0_gnn_in['W2'], 'L0_gnn_b2': _L0_gnn_in['b2'], 'L0_gnn_eps': _L0_gnn_in['eps'], 'L0_gnn_gamma': _L0_gnn_in['gamma'], 'L0_gnn_beta': _L0_gnn_in['beta'], 'L1_gnn_Wq': _L1_gnn_in['Wq'], 'L1_gnn_bq': _L1_gnn_in['bq'], 'L1_gnn_Wk': _L1_gnn_in['Wk'], 'L1_gnn_bk': _L1_gnn_in['bk'], 'L1_gnn_Wv': _L1_gnn_in['Wv'], 'L1_gnn_bv': _L1_gnn_in['bv'], 'L1_gnn_Wskip': _L1_gnn_in['Wskip'], 'L1_gnn_bskip': _L1_gnn_in['bskip'], 'L1_gnn_ln1_g': _L1_gnn_in['ln1_g'], 'L1_gnn_ln1_b': _L1_gnn_in['ln1_b'], 'L1_gnn_W1': _L1_gnn_in['W1'], 'L1_gnn_b1': _L1_gnn_in['b1'], 'L1_gnn_W2': _L1_gnn_in['W2'], 'L1_gnn_b2': _L1_gnn_in['b2'], 'L1_gnn_ln2_g': _L1_gnn_in['ln2_g'], 'L1_gnn_ln2_b': _L1_gnn_in['ln2_b']}

def reference(x, src, dst, L0_gnn_W1, L0_gnn_b1, L0_gnn_W2, L0_gnn_b2, L0_gnn_eps, L0_gnn_gamma, L0_gnn_beta, L1_gnn_Wq, L1_gnn_bq, L1_gnn_Wk, L1_gnn_bk, L1_gnn_Wv, L1_gnn_bv, L1_gnn_Wskip, L1_gnn_bskip, L1_gnn_ln1_g, L1_gnn_ln1_b, L1_gnn_W1, L1_gnn_b1, L1_gnn_W2, L1_gnn_b2, L1_gnn_ln2_g, L1_gnn_ln2_b):
    import jax
    import jax.numpy as jnp

    def _L0_gnn_ref(h, edge_index, W1, b1, W2, b2, eps, gamma, beta):
        import jax, jax.numpy as jnp
        import numpy as np
        N_NODES = 12500
        N_EDGES = 37500
        DIM = 256
        LN_EPS = 1e-05
        src, dst = (edge_index[0], edge_index[1])
        agg = jax.ops.segment_sum(h[src], dst, num_segments=h.shape[0])
        z = (1.0 + eps) * h + agg
        z = jax.nn.relu(z @ W1 + b1) @ W2 + b2
        r = z + h
        mu = jnp.mean(r, axis=-1, keepdims=True)
        var = jnp.mean(jnp.square(r - mu), axis=-1, keepdims=True)
        ln = (r - mu) * jax.lax.rsqrt(var + LN_EPS) * gamma + beta
        return jax.nn.relu(ln)

    def _L1_gnn_ref(x, edge_index, Wq, bq, Wk, bk, Wv, bv, Wskip, bskip, ln1_g, ln1_b, W1, b1, W2, b2, ln2_g, ln2_b):
        import jax, jax.numpy as jnp
        import numpy as np
        N = 2500
        E = 40000
        HID = 256
        H = 4
        D = HID // H
        FF = 4 * HID

        def _layernorm(x, g, b, eps=1e-05):
            mu = jnp.mean(x, axis=-1, keepdims=True)
            var = jnp.var(x, axis=-1, keepdims=True)
            return (x - mu) * jax.lax.rsqrt(var + eps) * g + b

        def _transformer_conv(x, edge_index, Wq, bq, Wk, bk, Wv, bv, Wskip, bskip):
            src, dst = (edge_index[0], edge_index[1])
            n = x.shape[0]
            q = (x @ Wq + bq).reshape(n, H, D)
            k = (x @ Wk + bk).reshape(n, H, D)
            v = (x @ Wv + bv).reshape(n, H, D)
            qi = q[dst]
            kj = k[src]
            vj = v[src]
            alpha = jnp.sum(qi * kj, axis=-1) / jnp.sqrt(jnp.float32(D))
            m = jax.ops.segment_max(alpha, dst, num_segments=n)
            ex = jnp.exp(alpha - m[dst])
            denom = jax.ops.segment_sum(ex, dst, num_segments=n)
            a = ex / (denom[dst] + 1e-16)
            out = jax.ops.segment_sum(a[..., None] * vj, dst, num_segments=n)
            out = out.reshape(n, H * D)
            return out + x @ Wskip + bskip
        x_new = _transformer_conv(x, edge_index, Wq, bq, Wk, bk, Wv, bv, Wskip, bskip)
        h = _layernorm(x + x_new, ln1_g, ln1_b)
        ffn = jax.nn.gelu(h @ W1 + b1, approximate=False) @ W2 + b2
        return _layernorm(h + ffn, ln2_g, ln2_b)
    edge_index = jnp.stack([src, dst])
    h = jnp.maximum(_layernorm(x, axis=-1), 0.0)
    x = x + _L0_gnn_ref(h, edge_index, L0_gnn_W1, L0_gnn_b1, L0_gnn_W2, L0_gnn_b2, L0_gnn_eps, L0_gnn_gamma, L0_gnn_beta)
    h = jnp.maximum(_layernorm(x, axis=-1), 0.0)
    x = x + _L1_gnn_ref(h, edge_index, L1_gnn_Wq, L1_gnn_bq, L1_gnn_Wk, L1_gnn_bk, L1_gnn_Wv, L1_gnn_bv, L1_gnn_Wskip, L1_gnn_bskip, L1_gnn_ln1_g, L1_gnn_ln1_b, L1_gnn_W1, L1_gnn_b1, L1_gnn_W2, L1_gnn_b2, L1_gnn_ln2_g, L1_gnn_ln2_b)
    return x

_drawn_inputs = setup_inputs


def setup_inputs(seed=0):
    import zlib

    import numpy as np

    out = dict(_drawn_inputs(seed))
    spreads = {'L0_gnn_b1': (0.0, 0.568),
     'L0_gnn_b2': (0.0, 0.406),
     'L0_gnn_gamma': (1.0, 0.2),
     'L0_gnn_beta': (0.0, 0.1),
     'L1_gnn_bq': (0.0, 0.8),
     'L1_gnn_bk': (0.0, 0.8),
     'L1_gnn_bv': (0.0, 0.1),
     'L1_gnn_bskip': (0.0, 0.1),
     'L1_gnn_ln1_g': (1.0, 0.2),
     'L1_gnn_ln1_b': (0.0, 0.1),
     'L1_gnn_b1': (0.0, 0.477),
     'L1_gnn_b2': (0.0, 0.1),
     'L1_gnn_ln2_g': (1.0, 0.2),
     'L1_gnn_ln2_b': (0.0, 0.1)}
    factors = {'L1_gnn_Wq': 8.0, 'L1_gnn_Wk': 8.0}
    for name, (base, spread) in spreads.items():
        noise = np.random.default_rng([zlib.crc32(name.encode()), seed]).standard_normal(out[name].shape)
        drawn = base * np.exp(spread * noise) if base else spread * noise
        out[name] = jnp.asarray(drawn.astype(out[name].dtype))
    for name, factor in factors.items():
        out[name] = (out[name] * factor).astype(out[name].dtype)
    return out
```

```python
from contextlib import ExitStack

import concourse.bass as bass
from concourse import mybir

N_NODES = 6250
N_EDGES = 100000
DIM = 256
HEADS = 4
HEAD_DIM = DIM // HEADS
FF = 4 * DIM
P = 128
TILES = -(-N_NODES // P)
TAIL = N_NODES - (TILES - 1) * P
CHUNK = 7
CHUNKS = TILES // CHUNK
KD = DIM // P
KF = FF // P
EDGE_TILES = -(-N_EDGES // P)
UNROLL = 16
GROUP = UNROLL // 2
STEPS = -(-(EDGE_TILES + TILES - 1) // UNROLL) * UNROLL
ROUNDS = STEPS // UNROLL
STEP_CHUNKS = -(-(STEPS + UNROLL) // P)
STEP_COLS = STEP_CHUNKS * P
LIST_ROWS = STEP_COLS + 1
SORT_ROWS = 125
SORT_COLS = N_EDGES // SORT_ROWS
DST_BITS = (N_NODES - 1).bit_length()
NO_NODE = 8191
ACC_W = DIM + HEADS
BIG = 1.5e38
EPS = 1e-5

assert SORT_ROWS * SORT_COLS == N_EDGES and SORT_COLS % GROUP == 0
assert CHUNKS * CHUNK == TILES and STEPS + UNROLL <= STEP_COLS


class Count:

    def __init__(self, eng, sem):
        self.eng, self.sem, self.base, self.k, self.j, self.per = eng, sem, 0, 0, None, 0

    def did(self, instruction):
        instruction.then_inc(self.sem, 1)
        self.k += 1

    def value(self):
        return self.base + self.k if self.j is None else self.j * self.per + (self.base + self.k)

    def settle(self):
        self.eng.wait_ge(self.sem, self.value())

    def enter(self, j, per):
        self.base, self.k, self.j, self.per = self.base + self.k, 0, j, per

    def leave(self, rounds):
        assert self.k == self.per, (self.k, self.per)
        self.base, self.k, self.j = self.base + rounds * self.per, 0, None


def gnn_kernel(nc, x, src, dst, l0, l1, out):
    f32, i32, bf16 = mybir.dt.float32, mybir.dt.int32, mybir.dt.bfloat16
    ALU, ACT, AX = mybir.AluOpType, mybir.ActivationFunctionType, mybir.AxisListType
    ds = bass.ds
    PE, DVE = mybir.EngineType.PE, mybir.EngineType.DVE

    with ExitStack() as ctx:
        def sb(name, shape, dt=f32):
            return ctx.enter_context(nc.sbuf_tensor(name, shape, dt))

        def sem(name):
            return ctx.enter_context(nc.semaphore(name))

        def dram(name, shape, dt=f32):
            return nc.dram_tensor(name, shape, dt, kind="Internal").ap()

        sorted_src = dram("sorted_src", [N_EDGES, 1], i32)
        sorted_dst = dram("sorted_dst", [N_EDGES, 1], i32)
        list_src = dram("list_src", [LIST_ROWS, P], i32)
        list_dst = dram("list_dst", [LIST_ROWS, P], i32)
        list_prev = dram("list_prev", [LIST_ROWS, P], i32)
        list_next = dram("list_next", [LIST_ROWS, P], i32)
        h0_rows = dram("h0_rows", [TILES * P, DIM])
        k_rows = dram("k_rows", [TILES * P, DIM])
        v_rows = dram("v_rows", [TILES * P, DIM])
        x1_rows = dram("x1_rows", [TILES * P, DIM])
        turn_rows = dram("turn_rows", [4, HEADS * STEP_CHUNKS * P])

        edge_pairs = dram("edge_pairs", [N_EDGES, 2], i32)

        region0 = sb("region0", [P, TILES * DIM])
        region1 = sb("region1", [P, TILES * ACC_W])
        region2 = sb("region2", [P, TILES * ACC_W])
        rows_buf = sb("rows_buf", [P, UNROLL * DIM])
        score = sb("score", [P, STEP_COLS * HEADS])
        src_step = sb("src_step", [P, STEP_COLS], mybir.dt.int16)
        dst_step = sb("dst_step", [P, STEP_COLS])
        break_fwd = sb("break_fwd", [P, STEP_COLS], bf16)
        break_rev = sb("break_rev", [P, STEP_COLS], bf16)
        off_tile = sb("off_tile", [P, STEP_COLS], bf16)
        index_ring = sb("index_ring", [P, UNROLL], i32)
        onehot = sb("onehot", [P, 4 * P])
        onehot_t = sb("onehot_t", [P, 4 * P])
        bias_rows = sb("bias_rows", [P, 7 * DIM])
        bias_cols = sb("bias_cols", [P, KF + KD])
        ident = sb("ident", [P, P])
        iota_row = sb("iota_row", [P, P])
        ones = sb("ones", [P, P], bf16)
        part_tile = sb("part_tile", [P, STEP_CHUNKS])
        bn6 = sb("bn6", [P, TILES * 6])
        rstd = sb("rstd", [P, TILES])
        neg_mean = sb("neg_mean", [P, TILES])
        eps_gin = sb("eps_gin", [P, 2])
        node_tile = sb("node_tile", [1, STEP_COLS], i32)
        row_sum = sb("row_sum", [P, (2 * HEADS + 2) * STEP_CHUNKS])
        ln_tmp = sb("ln_tmp", [P, 4 * TILES])
        mean2, diff, variance, diff2 = (ln_tmp[:, c * TILES:(c + 1) * TILES] for c in range(4))
        denom = ln_tmp

        psum = [ctx.enter_context(nc.psum_tensor(f"bank{b}", [P, 512], f32)) for b in range(8)]

        def tiles(region, width=DIM):
            return region[:, 0:TILES * width].rearrange("p (t w) -> p t w", w=width)

        attn = tiles(region2, ACC_W)

        def chunk(region, j, width=DIM, keep=DIM):
            v = region[:, ds(j * (CHUNK * width), CHUNK * width)]
            return v.rearrange("p (t w) -> p t w", w=width)[:, :, 0:keep]

        def tile_of(region, j, u, width=DIM, keep=DIM):
            return region[:, ds(j * (CHUNK * width) + u * width, keep)]

        def col(t, j, u, n=1, stride=1, off=0):
            return t[:, ds(j * (CHUNK * stride) + u * stride + off, n)]

        def bias(n):
            return bias_rows[:, n * DIM:(n + 1) * DIM]

        def bias_over_chunk(n):
            return bias(n).unsqueeze(1).to_broadcast([P, CHUNK, DIM])

        at = [0]

        def work(n, dt=f32):
            size = n if dt != bf16 else n // 2
            v = region2[:, at[0]:at[0] + size]
            at[0] += size
            return v if dt == f32 else v.bitcast(dt)

        iota_i = work(STEP_COLS, i32)
        iota_step = work(STEP_COLS)
        part_i = work(STEP_CHUNKS, i32)
        first_i = work(STEP_CHUNKS, i32)
        first_t = work(STEP_CHUNKS, i32)
        leave = work(STEP_CHUNKS)
        edge_tile_f = work(STEP_CHUNKS)
        edge_tile_i = work(STEP_CHUNKS, i32)
        node_tile_128 = work(STEP_CHUNKS)
        left = work(STEP_CHUNKS * STEP_COLS, bf16)
        row_src = work(STEP_COLS, i32)
        row_dst = work(STEP_COLS, i32)
        row_prev = work(STEP_COLS, i32)
        row_next = work(STEP_COLS, i32)
        src_f = work(STEP_COLS)
        dst_f = work(STEP_COLS)
        valid = work(STEP_COLS)
        differs = work(STEP_COLS)
        step_f = differs
        pad_node = work(P, i32)
        pad_zero = work(P, i32)
        pad_first = work(1, i32)
        assert at[0] <= TILES * ACC_W

        SR = SORT_ROWS
        def sort_work(t, n, width=1, dt=f32):
            v = t[0:SR, n * SORT_COLS:(n + width) * SORT_COLS]
            return v if dt == f32 else v.bitcast(dt)
        dst_here = sort_work(score, 0, dt=i32)
        dst_after = sort_work(score, 1, dt=i32)
        descends = sort_work(score, 2)
        src_here = sort_work(score, 3, dt=i32)
        pairs = sort_work(rows_buf, 0, 2, i32).rearrange("p (c w) -> p c w", w=2)
        digit = sort_work(rows_buf, 2)
        digits_before = sort_work(rows_buf, 3)
        place_i = sort_work(rows_buf, 4, dt=i32)
        place = descends
        place_one = dst_after.bitcast(f32)
        earlier = onehot[0:SR, 0:SR]
        ones_f = onehot[0:SR, P:P + SR]
        sort_cols = onehot[0:SR, 2 * P:2 * P + 8]
        digit_mask = onehot[0:SR, 2 * P + 8:2 * P + 9].bitcast(i32)
        pair_stage = onehot[0:SR, 3 * P:3 * P + 2 * GROUP].bitcast(i32)
        place_stage = onehot[0:SR, 3 * P + 32:3 * P + 32 + GROUP].bitcast(i32)
        unsorted = onehot_t[0:1, 0:1].bitcast(i32)

        SC = STEP_COLS
        score_rows = region1[:, 0:HEADS * SC]
        fwd = region1[:, HEADS * SC:2 * HEADS * SC]
        rev = region1[:, 2 * HEADS * SC:3 * HEADS * SC]
        open_fwd = region1[:, 3 * HEADS * SC:3 * HEADS * SC + SC]
        open_rev = region1[:, 3 * HEADS * SC + SC:3 * HEADS * SC + 2 * SC]
        carried = score[:, 0:HEADS * SC]
        reset_fwd = bias_rows[:, 0:SC]
        reset_rev = bias_rows[:, SC:2 * SC]
        inner_fwd = onehot[:, 0:SC // 2].bitcast(bf16)
        inner_rev = onehot_t[:, 0:SC // 2].bitcast(bf16)
        HC = HEADS * STEP_CHUNKS
        sum_t = [rows_buf[0:HC, 0:P], rows_buf[0:HC, P:2 * P],
                 rows_buf[0:STEP_CHUNKS, 2 * P:3 * P], rows_buf[0:STEP_CHUNKS, 3 * P:4 * P]]
        line_val = [rows_buf[0:HEADS, 4 * P + n * SC:4 * P + (n + 1) * SC] for n in range(2)]
        line_brk = [rows_buf[0:HEADS, 4 * P + (2 + n) * SC:4 * P + (3 + n) * SC] for n in range(2)]
        line_out = [score[0:HEADS, n * SC:(n + 1) * SC] for n in range(2)]
        score3 = score[:, :].rearrange("p (s h) -> p s h", h=HEADS)
        TURNS = [(h, c, min(4, STEP_CHUNKS - c)) for h in range(HEADS) for c in range(0, STEP_CHUNKS, 4)]

        rows = rows_buf[:, :].rearrange("p (b w) -> p b w", w=DIM)
        w1_gin = rows_buf[:, 0:KD * DIM].rearrange("p (k n) -> p k n", k=KD)
        w2_gin = rows_buf[:, KD * DIM:2 * KD * DIM].rearrange("p (k n) -> p k n", k=KD)
        w_proj = rows_buf[:, 2 * KD * DIM:2 * KD * DIM + KD * 4 * DIM].rearrange("p (k n) -> p k n", k=KD)
        w_up = rows_buf[:, 0:KD * FF].rearrange("p (k n) -> p k n", k=KD)
        w_down = rows_buf[:, KD * FF:KD * FF + KF * DIM].rearrange("p (k n) -> p k n", k=KF)
        kv_stage = score[:, :].rearrange("p (t w) -> p t w", w=2 * DIM)
        z_ring = score[:, 0:CHUNK * DIM].rearrange("p (t w) -> p t w", w=DIM)
        h_ring = z_ring
        u_ring, h1_ring, h1t_ring = (region1[:, n * CHUNK * DIM:(n + 1) * CHUNK * DIM].rearrange("p (t w) -> p t w", w=DIM)
                                     for n in range(3))
        gelu_t = score[:, 0:2 * FF].rearrange("p (s f n) -> p s f n", s=2, n=P)

        BANKS = {0: CHUNK, 1: 3, 2: 3, 3: 1, 4: 2, 5: CHUNK, 6: 2}

        s_const = sem("const_ready")
        s_dve = sem("dve_done")
        s_x = sem("x_loaded")
        s_wload = sem("weights_loaded")
        s_lists = sem("edge_lists_copied")
        s_sorted = sem("sorted_edges_written")
        s_checkload = sem("check_lists_loaded")
        s_after = sem("padded_successors")
        s_descents = sem("descents_counted_by_row")
        s_check = sem("descents_summed")
        s_flag = sem("sorted_flag_ready")
        s_srcload = sem("sources_loaded")
        s_pairs = sem("pairs_loaded")
        s_digits = sem("digits_counted")
        s_prefix = sem("digit_prefix_ready")
        s_place = sem("places_ready")
        s_stage = sem("pairs_staged")
        s_scatter = [sem(f"pairs_scattered{c}") for c in range(GROUP)]
        s_split = sem("pairs_split")
        s_sort = sem("sort_steps")
        s_first = sem("first_destinations_loaded")
        s_left = sem("left_masks_ready")
        s_stair = sem("staircase_summed")
        s_index = sem("row_indices_ready")
        s_rowload = sem("edge_rows_gathered")
        s_tables = sem("row_tables_ready")
        s_turned = sem("tables_turned")
        s_steps = sem("step_tables_ready")
        s_offsets = sem("tile_offsets_ready")
        s_weighted = sem("values_weighted")
        s_hready = sem("ffn_input_ready")
        s_sums = sem("row_ends_ready")
        s_sumturn = sem("row_ends_turned")
        s_log = sem("exponents_ready")
        s_eps = sem("eps_loaded")
        s_bias = sem("biases_loaded")
        s_zero1 = sem("aggregate_zeroed")
        s_stats = sem("layernorm_stats_ready")
        s_var = sem("layernorm_variance_ready")
        s_std = sem("layernorm_deviation_ready")
        s_rstd = sem("layernorm_rstd_ready")
        s_norm = sem("normalised")
        s_h0 = sem("h0_stored")
        s_ring = sem("indices_copied")
        s_row = [sem(f"row_gathered{b}") for b in range(UNROLL)]
        s_used = [sem(f"row_used{n}") for n in range(3)]
        s_hot = [sem(f"onehot_ready{n}") for n in range(3)]
        s_part = [sem(f"partial_ready{n}") for n in range(3)]
        s_added = [sem(f"partial_added{n}") for n in range(3)]
        s_flip = sem("onehot_turned")
        s_flipped = sem("onehot_t_ready")
        s_z = sem("z_ready")
        s_h1 = sem("h1_ready")
        s_res1 = sem("h1_kept")
        s_up = [sem(f"stage_psum_ready{n}") for n in range(8)]
        s_ev = [sem(f"stage_evacuated{n}") for n in range(8)]
        s_xr = sem("x_reloaded")
        s_x1 = sem("x1_ready")
        s_x1st = sem("x1_stored")
        s_kv = [sem(f"kv_stored{b}") for b in range(CHUNK)]
        s_kvready = sem("kv_staged")
        s_sm = sem("softmax_turned")
        s_smev = sem("softmax_evacuated")
        s_rowsum = sem("row_summaries_ready")
        s_rowdma = sem("row_summaries_moved")
        s_carry = sem("carries_ready")
        s_zero2 = sem("sums_zeroed")
        s_exp = sem("weights_ready")
        s_hkept = sem("ffn_input_kept")
        s_gelu = sem("gelu_ready")
        s_gup = sem("hidden_psum_ready")
        s_res = sem("residual_ready")
        s_y = sem("output_ready")
        s_out = sem("output_stored")

        TAIL_ZERO, PADS, IOTAS = 1, 4, 6

        block = ctx.enter_context(nc.Block())

        def node_tiles(engine_type, j, half):
            _, v = nc.values_load_multi_w_load_instructions(
                node_tile[0:1, ds(j * UNROLL + half * GROUP, GROUP)], engines=[engine_type], min_val=0,
                max_val=TILES - 1, skip_runtime_bounds_check_because="the table is clamped to the tile count")
            return v

        def if_unsorted(eng, engine_type):
            eng.wait_ge(s_flag, 1)
            _, v = nc.values_load_multi_w_load_instructions(
                unsorted, engines=[engine_type], min_val=0, max_val=1,
                skip_runtime_bounds_check_because="a comparison's result")
            return eng.If(v[0])

        @block.sync
        def _(sp):
            def load_x(region, s, base):
                sp.dma_start(region[0:TAIL, (TILES - 1) * DIM:TILES * DIM], x[(TILES - 1) * P:N_NODES, :]).then_inc(s, 16)
                sp.wait_ge(s, base + 16)
                with sp.Fori(0, CHUNKS - 1) as j:
                    sp.dma_start(chunk(region, j),
                                 x[ds(j * (CHUNK * P), CHUNK * P), :].rearrange("(t p) f -> p t f", p=P)).then_inc(s, 16)
                    sp.wait_ge(s, j * 16 + (base + 32))
                    sp.nop(nofuse=True)
                t0 = (CHUNKS - 1) * CHUNK
                full = region[:, t0 * DIM:(TILES - 1) * DIM].rearrange("p (t w) -> p t w", w=DIM)
                sp.dma_start(full, x[t0 * P:(TILES - 1) * P, :].rearrange("(t p) f -> p t f", p=P)).then_inc(s, 16)

            flat_rows = lambda t, a, n: t[a:a + n * SORT_COLS].rearrange("(p c) -> p c", c=SORT_COLS)
            sp.dma_start(dst_here, flat_rows(dst, 0, SR)).then_inc(s_checkload, 16)
            sp.wait_ge(s_after, 1)
            sp.dma_start(dst_after[0:SR - 1, :], flat_rows(dst, 1, SR - 1)).then_inc(s_checkload, 16)
            sp.dma_start(dst_after[SR - 1:SR, 0:SORT_COLS - 1],
                         dst[(SR - 1) * SORT_COLS + 1:N_EDGES].rearrange("(a b) -> a b", a=1)).then_inc(s_checkload, 16)

            sp.wait_ge(s_const, TAIL_ZERO)
            load_x(region0, s_x, 0)

            with sp.Fori(0, CHUNKS) as j:
                sp.wait_ge(s_norm, j + 1)
                sp.nop(nofuse=True)
                sp.dma_start(h0_rows[ds(j * (CHUNK * P), CHUNK * P), :].rearrange("(t p) f -> p t f", p=P),
                             chunk(region0, j)).then_inc(s_h0, 16)

            sp.wait_ge(s_part[0], STEPS)
            def w_view(w):
                return w.rearrange("(k p) n -> p k n", p=P)
            loads = [(w1_gin, w_view(l0["W1"])), (w2_gin, w_view(l0["W2"])),
                     (w_proj[:, :, 0:DIM], w_view(l1["Wq"])), (w_proj[:, :, DIM:2 * DIM], w_view(l1["Wk"])),
                     (w_proj[:, :, 2 * DIM:3 * DIM], w_view(l1["Wv"])),
                     (w_proj[:, :, 3 * DIM:4 * DIM], w_view(l1["Wskip"]))]
            for d, s in loads:
                sp.dma_start(d, s).then_inc(s_wload, 16)

            sp.wait_ge(s_up[1], TILES)
            sp.wait_ge(s_xr, 1)
            load_x(region2, s_xr, 1)

            with sp.Fori(0, CHUNKS) as j:
                sp.wait_ge(s_x1, j + 1)
                sp.nop(nofuse=True)
                sp.dma_start(x1_rows[ds(j * (CHUNK * P), CHUNK * P), :].rearrange("(t p) f -> p t f", p=P),
                             chunk(region2, j)).then_inc(s_x1st, 16)

            with sp.Fori(0, CHUNKS) as j:
                for u in range(CHUNK):
                    sp.wait_ge(s_kvready, j * CHUNK + (u + 1))
                    sp.nop(nofuse=True)
                    at_rows = ds(j * (CHUNK * P) + u * P, P)
                    sp.dma_start(k_rows[at_rows, :], kv_stage[:, u, 0:DIM]).then_inc(s_kv[u], 16)
                    sp.dma_start(v_rows[at_rows, :], kv_stage[:, u, DIM:2 * DIM]).then_inc(s_kv[u], 16)

            sp.wait_ge(s_rowsum, 1)
            for n in range(2):
                sp.dma_start(turn_rows[n, :].rearrange("(r p) -> r p", p=P), sum_t[n]).then_inc(s_rowdma, 16)
                sp.dma_start(turn_rows[2 + n, 0:SC].rearrange("(r p) -> r p", p=P), sum_t[2 + n]).then_inc(s_rowdma, 16)
            sp.wait_ge(s_rowdma, 64)
            for n in range(2):
                sp.dma_start(line_val[n], turn_rows[n, :].rearrange("(h s) -> h s", h=HEADS)).then_inc(s_rowdma, 16)
                sp.dma_start(line_brk[n], turn_rows[2 + n, 0:SC].partition_broadcast(HEADS)).then_inc(s_rowdma, 16)
            sp.wait_ge(s_carry, 1)
            for n in range(2):
                sp.dma_start(turn_rows[n, :].rearrange("(h s) -> h s", h=HEADS), line_out[n]).then_inc(s_rowdma, 16)
            sp.wait_ge(s_rowdma, 160)
            for n in range(2):
                sp.dma_start(sum_t[n], turn_rows[n, :].rearrange("(r p) -> r p", p=P)).then_inc(s_rowdma, 16)

            sp.wait_ge(s_part[2], STEPS)
            sp.dma_start(w_up, l1["W1"].rearrange("(k p) n -> p k n", p=P)).then_inc(s_wload, 16)
            sp.dma_start(w_down, l1["W2"].rearrange("(k p) n -> p k n", p=P)).then_inc(s_wload, 16)
            sp.wait_ge(s_res, CHUNKS)
            sp.wait_ge(s_x1st, 16 * CHUNKS)
            with sp.Fori(0, CHUNKS) as j:
                sp.dma_start(chunk(region2, j),
                             x1_rows[ds(j * (CHUNK * P), CHUNK * P), :].rearrange("(t p) f -> p t f", p=P)).then_inc(s_x1, 16)
                sp.wait_ge(s_x1, j * 16 + (CHUNKS + 16))
                sp.nop(nofuse=True)
            with sp.Fori(0, CHUNKS - 1) as j:
                sp.wait_ge(s_y, j + 1)
                sp.nop(nofuse=True)
                sp.dma_start(out[ds(j * (CHUNK * P), CHUNK * P), :].rearrange("(t p) f -> p t f", p=P),
                             chunk(region0, j)).then_inc(s_out, 16)
            t0 = (CHUNKS - 1) * CHUNK
            sp.wait_ge(s_y, CHUNKS)
            sp.dma_start(out[t0 * P:(TILES - 1) * P, :].rearrange("(t p) f -> p t f", p=P),
                         region0[:, t0 * DIM:(TILES - 1) * DIM].rearrange("p (t w) -> p t w", w=DIM)).then_inc(s_out, 16)
            sp.dma_start(out[(TILES - 1) * P:N_NODES, :],
                         region0[0:TAIL, (TILES - 1) * DIM:TILES * DIM]).then_inc(s_out, 16)
            sp.wait_ge(s_out, 16 * (CHUNKS + 1))


        @block.gpsimd
        def _(pool):
            tail_from = TAIL // 32 * 32
            def constant(instruction, n):
                instruction.then_inc(s_const, 1)
                pool.wait_ge(s_const, n)

            constant(pool.memset(region0[tail_from:P, (TILES - 1) * DIM:TILES * DIM], 0.0), TAIL_ZERO)
            constant(pool.memset(pad_node, NO_NODE), 2)
            constant(pool.memset(pad_zero, 0), 3)
            constant(pool.memset(pad_first, -1), PADS)
            constant(pool.iota(iota_i, [[1, STEP_COLS]], base=0, channel_multiplier=0), 5)
            constant(pool.iota(part_i, [[P, STEP_CHUNKS]], base=0, channel_multiplier=1), IOTAS)
            pool.memset(region1[:, 0:TILES * ACC_W], 0.0).then_inc(s_zero1, 1)
            pool.wait_ge(s_zero1, 1)

            with if_unsorted(pool, mybir.EngineType.Pool):
                pool.dma_start(src_here, src.rearrange("(p c) -> p c", c=SORT_COLS)).then_inc(s_srcload, 16)
                with pool.Fori(0, DST_BITS) as bit:
                    pool.wait_ge(s_place, bit + 1)
                    pool.nop(nofuse=True)
                    with pool.Fori(0, SORT_COLS // GROUP) as g:
                        n = bit * (SORT_COLS // GROUP) + g
                        pool.tensor_copy(pair_stage, rows_buf[0:SR, ds(g * (2 * GROUP), 2 * GROUP)].bitcast(i32)).then_inc(s_stage, 1)
                        pool.wait_ge(s_stage, n * 2 + 1)
                        pool.tensor_copy(place_stage, rows_buf[0:SR, ds(g * GROUP + 4 * SORT_COLS, GROUP)].bitcast(i32)).then_inc(s_stage, 1)
                        pool.wait_ge(s_stage, n * 2 + 2)
                        pool.nop(nofuse=True)
                        for c in range(GROUP):
                            pool.indirect_dma_start(edge_pairs, bass.IndirectOffsetOnAxis(ap=place_stage[:, c:c + 1], axis=0),
                                                    pair_stage[:, 2 * c:2 * c + 2], None).then_inc(s_scatter[c], 16)
                        for c in range(GROUP):
                            pool.wait_ge(s_scatter[c], n * 16 + 16)
                            pool.nop(nofuse=True)
                    pool.dma_start(rows_buf[0:SR, 0:2 * SORT_COLS].bitcast(i32),
                                   edge_pairs.rearrange("(p c) w -> p (c w)", p=SR)).then_inc(s_pairs, 16)
                pool.wait_ge(s_split, 1)
                pool.dma_start(sorted_dst.rearrange("(p c) o -> p (c o)", p=SR), dst_here).then_inc(s_sorted, 16)
                pool.dma_start(sorted_src.rearrange("(p c) o -> p (c o)", p=SR), src_here).then_inc(s_sorted, 16)
            with pool.Else():
                for to, fr in ((sorted_src, src), (sorted_dst, dst)):
                    pool.dma_start(to.rearrange("(a b) o -> a (b o)", a=16), fr.rearrange("(a b) -> a b", a=16)).then_inc(s_sorted, 16)

            pool.wait_ge(s_index, 1)
            pool.wait_ge(s_lists, 16 * 13)
            for c in range(STEP_CHUNKS):
                for table, rows_out in ((list_src, row_src), (list_dst, row_dst), (list_prev, row_prev), (list_next, row_next)):
                    pool.indirect_dma_start(rows_out[:, c * P:(c + 1) * P], None, table,
                                            bass.IndirectOffsetOnAxis(ap=edge_tile_i[:, c:c + 1], axis=0)).then_inc(s_rowload, 16)

            def gather(n, table, used):
                def group(j, half, first):
                    g0 = half * GROUP
                    if not first:
                        pool.wait_ge(used, j * UNROLL + (g0 + GROUP - UNROLL))
                    pool.tensor_copy(index_ring[:, g0:g0 + GROUP],
                                     src_step[:, ds(j * UNROLL + g0, GROUP)]).then_inc(s_ring, 1)
                    pool.wait_ge(s_ring, j * 2 + (2 * ROUNDS * n + half + 1))
                    pool.nop(nofuse=True)
                    for b in range(g0, g0 + GROUP):
                        pool.indirect_dma_start(rows[:, b, :], None, table,
                                                bass.IndirectOffsetOnAxis(ap=index_ring[:, b:b + 1], axis=0)).then_inc(s_row[b], 16)
                group(0, 0, True)
                group(0, 1, True)
                with pool.Fori(1, ROUNDS) as j:
                    group(j, 0, False)
                    group(j, 1, False)

            pool.wait_ge(s_steps, 2)
            pool.wait_ge(s_h0, 16 * CHUNKS)
            gather(0, h0_rows, s_part[0])

            pool.wait_ge(s_up[1], TILES)
            pool.memset(region2[tail_from:P, (TILES - 1) * DIM:TILES * DIM], 0.0).then_inc(s_xr, 1)

            for b in range(CHUNK):
                pool.wait_ge(s_kv[b], 32 * CHUNKS)
            pool.wait_ge(s_up[4], 2 * TILES + 2 * CHUNK)
            gather(1, k_rows, s_used[1])

            pool.wait_ge(s_part[1], STEPS)
            pool.memset(region2[:, 0:TILES * ACC_W], 0.0).then_inc(s_zero2, 1)
            pool.wait_ge(s_sumturn, 2)
            pool.wait_ge(s_used[1], STEPS)
            gather(2, v_rows, s_part[2])

        @block.scalar
        def _(act):
            for n in (0, 1, 3, 5):
                act.sem_inc(s_ev[n], BANKS[n])
            act.sem_inc(s_gelu, 2)
            flat = lambda t: t.rearrange("a b -> (a b)")
            act.wait_ge(s_sorted, 32)
            act.wait_ge(s_const, PADS)
            spans = [(list_src, sorted_src, 0, 0, N_EDGES, pad_zero), (list_dst, sorted_dst, 0, 0, N_EDGES, pad_node),
                     (list_prev, sorted_dst, 1, 0, N_EDGES, pad_node), (list_next, sorted_dst, 0, 1, N_EDGES - 1, pad_node)]
            total = LIST_ROWS * P
            for t, s, to, fr, n, pad in spans:
                tf, sf = flat(t), flat(s)
                act.dma_start(tf[to:to + n], sf[fr:fr + n]).then_inc(s_lists, 16)
                end = to + n
                whole = (total - end) // P * P
                act.dma_start(tf[end:total - whole].rearrange("(a b) -> a b", a=1),
                              pad[0:1, 0:total - whole - end]).then_inc(s_lists, 16)
                act.dma_start(tf[total - whole:total].rearrange("(a b) -> a b", b=P), pad[0:whole // P, :]).then_inc(s_lists, 16)
            act.dma_start(flat(list_prev)[0:1].rearrange("(a b) -> a b", a=1), pad_first[0:1, :]).then_inc(s_lists, 16)
            act.wait_ge(s_lists, 16 * 13)
            act.dma_start(first_i, list_dst[1:STEP_COLS + 1, 0:1].rearrange("(c p) o -> p (c o)", p=P),
                          allow_slow_non_contiguous=True).then_inc(s_first, 16)
            act.dma_start(eps_gin[:, 0:1], l0["eps"].partition_broadcast(P)).then_inc(s_eps, 16)
            row = lambda v: v.partition_broadcast(P)
            for n, v in enumerate((l0["b2"], l0["gamma"], l0["beta"], l1["bq"], l1["bk"], l1["bv"], l1["bskip"])):
                act.dma_start(bias(n), row(v)).then_inc(s_bias, 16)
            act.dma_start(bias_cols[:, 0:KD], l0["b1"].rearrange("(c p) -> p c", p=P), allow_slow_non_contiguous=True).then_inc(s_bias, 16)
            act.dma_start(bias_cols[:, KD:KD + KF], l1["b1"].rearrange("(c p) -> p c", p=P), allow_slow_non_contiguous=True).then_inc(s_bias, 16)

            def norm_tile(dest, source, func, j, u):
                return act.activation(dest, tile_of(source, j, u), func, scale=col(rstd, j, u), bias=col(neg_mean, j, u))

            def norm_factors(n):
                act.wait_ge(s_var, n + 1)
                act.activation(variance, variance, ACT.Sqrt).then_inc(s_std, 1)
                act.wait_ge(s_rstd, n + 1)

            def normalise(n, source, func):
                norm_factors(n)
                with act.Fori(0, CHUNKS) as j:
                    for u in range(CHUNK):
                        last = norm_tile(tile_of(region0, j, u), source, func, j, u)
                    last.then_inc(s_norm, 1)

            normalise(0, region0, ACT.Relu)

            def evacuate_transposed(n, dest):
                with act.Fori(0, CHUNKS) as j:
                    for u in range(CHUNK):
                        act.wait_ge(s_up[n], j * CHUNK + (CHUNK + u + 1))
                        act.activation(tile_of(dest, j, u), psum[u][:, 0:DIM], ACT.Copy).then_inc(s_ev[n], 1)

            act.wait_ge(s_bias, 16 * 9)
            evacuate_transposed(0, region2)
            with act.Fori(0, CHUNKS) as j:
                for u in range(CHUNK):
                    act.wait_ge(s_up[1], j * CHUNK + (u + 1))
                    act.wait_ge(s_up[2], j * CHUNK + (u + 1))
                    for k in range(KD):
                        last = act.activation(u_ring[:, u, k * P:(k + 1) * P], psum[u % 4][:, k * P:(k + 1) * P],
                                              ACT.Relu, bias=bias_cols[:, k:k + 1])
                    last.then_inc(s_ev[1], 1)
            normalise(1, region0, ACT.Identity)
            norm_factors(2)
            with act.Fori(0, CHUNKS) as j:
                for u in range(CHUNK + 1):
                    if u < CHUNK:
                        act.wait_ge(s_up[3], j * CHUNK + (u + 1))
                        act.wait_ge(s_res1, j * CHUNK + (u + 1))
                        last = norm_tile(h1_ring[:, u, :], region2, ACT.Relu, j, u)
                        last.then_inc(s_h1, 1)
                    if u:
                        v = u - 1
                        act.wait_ge(s_up[3], j * CHUNK + (CHUNK + v + 1))
                        act.wait_ge(s_up[4], j * (2 * CHUNK) + (2 * v + 2))
                        act.activation(h1t_ring[:, v, :], psum[v % 2][:, 0:DIM], ACT.Copy).then_inc(s_ev[3], 1)
                act.sem_inc(s_norm, 1)

            with act.Fori(0, ROUNDS) as j:
                for u in range(UNROLL):
                    act.wait_ge(s_flip, j * UNROLL + (u + 1))
                    o = u % 4 * P
                    act.activation(onehot_t[:, o:o + P], psum[4 + u % 2][:, 0:P], ACT.Copy).then_inc(s_flipped, 1)

            act.wait_ge(s_carry, 1)
            for n, v in enumerate((l1["b2"], l1["ln1_g"], l1["ln1_b"], l1["ln2_g"], l1["ln2_b"])):
                act.dma_start(bias(n), row(v)).then_inc(s_bias, 16)
            for h in range(HEADS):
                act.wait_ge(s_log, h + 1)
                act.activation(score_rows[:, h * SC:(h + 1) * SC], fwd[:, h * SC:(h + 1) * SC], ACT.Exp,
                               scale=HEAD_DIM ** -0.5).then_inc(s_exp, 1)

            act.wait_ge(s_smev, len(TURNS))
            with act.Fori(0, ROUNDS) as j:
                for u in range(UNROLL):
                    act.wait_ge(s_row[u], j * 16 + (32 * ROUNDS + 16))
                    for h in range(HEADS):
                        part = rows[:, u, h * HEAD_DIM:(h + 1) * HEAD_DIM]
                        last = act.activation(part, part, ACT.Copy, scale=score[:, ds(j * (UNROLL * HEADS) + u * HEADS + h, 1)])
                    last.then_inc(s_weighted, 1)

            normalise(3, region0, ACT.Identity)
            evacuate_transposed(5, region1)

            act.wait_ge(s_hkept, 1)
            def gelu(t, slot):
                act.wait_ge(s_gup, t + 1)
                act.wait_ge(s_up[6], t + 1)
                for f in range(KF):
                    last = act.activation(gelu_t[:, slot, f, :], psum[2 * slot + f // 4][:, f % 4 * P:(f % 4 + 1) * P],
                                          ACT.Gelu, bias=bias_cols[:, KD + f:KD + f + 1])
                last.then_inc(s_gelu, 1)
            with act.Fori(0, TILES // 2) as i:
                gelu(i * 2, 0)
                gelu(i * 2 + 1, 1)
            gelu(TILES - 1, 0)
            normalise(4, region0, ACT.Identity)

        @block.tensor
        def _(pe):
            mm = nc.tensor.matmul
            for n in (0, 2, 3, 5):
                pe.sem_inc(s_up[n], CHUNK)
            pe.sem_inc(s_up[4], 2 * CHUNK)
            pe.sem_inc(s_up[6], 2)
            pe.wait_ge(s_descents, 1)
            mm(psum[0][0:1, 0:1], sort_cols[:, 0:1], ones_f[:, 0:1], start=True, stop=True).then_inc(s_check, 1)
            with if_unsorted(pe, PE):
                with pe.Fori(0, DST_BITS) as bit:
                    pe.wait_ge(s_digits, bit + 1)
                    ends = digits_before[:, SORT_COLS - 1:SORT_COLS]
                    mm(psum[0][0:SR, 0:1], earlier, ends, start=True, stop=True)
                    mm(psum[0][0:SR, 1:2], ones_f, ends, start=True, stop=True).then_inc(s_prefix, 1)
            pe.wait_ge(s_left, STEP_CHUNKS)
            left3 = left.rearrange("p (c s) -> p c s", c=STEP_CHUNKS)
            half = SC // 2
            for b in range(2):
                for c in range(STEP_CHUNKS):
                    last = mm(psum[b][0:1, 0:half], ones[:, 0:1], left3[:, c, b * half:(b + 1) * half],
                              start=c == 0, stop=c == STEP_CHUNKS - 1)
            for o in range(STEP_CHUNKS):
                for c in range(STEP_CHUNKS):
                    last = mm(psum[2][:, o:o + 1], left3[:, c, o * P:(o + 1) * P], ones[:, 0:1],
                              start=c == 0, stop=c == STEP_CHUNKS - 1)
            last.then_inc(s_stair, 1)
            pe.wait_ge(s_tables, 1)
            for n, t in enumerate((src_f, dst_f)):
                for c in range(STEP_CHUNKS):
                    last = nc.tensor.transpose(psum[3 + 2 * n + c // 4][:, c % 4 * P:(c % 4 + 1) * P], t[:, c * P:(c + 1) * P], ident[:, :])
            last.then_inc(s_turned, 1)

            def sum_pass(n):
                pe.wait_ge(s_steps, 2)
                with pe.Fori(0, ROUNDS) as j:
                    for u in range(UNROLL):
                        o = u % 4 * P
                        pe.wait_ge(s_hot[n], j * UNROLL + (u + 1))
                        if n == 0:
                            pe.wait_ge(s_row[u], j * 16 + 16)
                        else:
                            pe.wait_ge(s_weighted, j * UNROLL + (u + 1))
                        pe.wait_ge(s_added[n], j * UNROLL + (u + 1))
                        last = mm(psum[u % 4][:, 0:DIM], onehot[:, o:o + P], rows[:, u, :], start=True, stop=True)
                        if n == 2:
                            last = mm(psum[u % 4][:, DIM:ACC_W], onehot[:, o:o + P],
                                      score[:, ds(j * (UNROLL * HEADS) + u * HEADS, HEADS)], start=True, stop=True)
                        last.then_inc(s_part[n], 1)

            sum_pass(0)

            def transpose_tile(dest, place):
                for k in range(KD):
                    last = nc.tensor.transpose(dest[:, k * P:(k + 1) * P], place[:, k * P:(k + 1) * P], ident[:, :])
                return last

            def transpose_stage(n, ring, ready):
                with pe.Fori(0, CHUNKS) as j:
                    for u in range(CHUNK):
                        pe.wait_ge(ready, j * CHUNK + (u + 1))
                        pe.wait_ge(s_ev[n], j * CHUNK + (u + 1))
                        transpose_tile(psum[u], ring[:, u, :]).then_inc(s_up[n], 1)
                pe.wait_ge(s_ev[n], TILES + BANKS[n])

            pe.wait_ge(s_added[0], STEPS + 4)
            transpose_stage(0, z_ring, s_z)
            pe.wait_ge(s_wload, 16 * 6)
            with pe.Fori(0, CHUNKS) as j:
                for u in range(CHUNK + 1):
                    if u < CHUNK:
                        pe.wait_ge(s_ev[1], j * CHUNK + (u + 1))
                        for f in range(KD):
                            for k in range(KD):
                                last = mm(psum[u % 4][:, f * P:(f + 1) * P], w1_gin[:, k, f * P:(f + 1) * P],
                                          region2[:, ds(j * (CHUNK * DIM) + (u * DIM + k * P), P)], start=k == 0, stop=k == KD - 1)
                        last.then_inc(s_up[1], 1)
                    if u:
                        v = u - 1
                        pe.wait_ge(s_ev[1], j * CHUNK + (v + 1 + BANKS[1]))
                        pe.wait_ge(s_ev[2], j * CHUNK + (v + 1))
                        for k in range(KD):
                            last = mm(psum[4 + v % 4][:, 0:DIM], u_ring[:, v, k * P:(k + 1) * P], w2_gin[:, k, :],
                                      start=k == 0, stop=k == KD - 1)
                        last.then_inc(s_up[2], 1)
            pe.wait_ge(s_ev[2], TILES + BANKS[2])
            with pe.Fori(0, CHUNKS) as j:
                for u in range(CHUNK + 1):
                    if u < CHUNK:
                        pe.wait_ge(s_h1, j * CHUNK + (u + 1))
                        pe.wait_ge(s_ev[3], j * CHUNK + (u + 1))
                        transpose_tile(psum[u % 2], h1_ring[:, u, :]).then_inc(s_up[3], 1)
                    if u:
                        v = u - 1
                        pe.wait_ge(s_ev[3], j * CHUNK + (v + 1 + BANKS[3]))
                        for side in range(2):
                            unit = 2 * v + side
                            pe.wait_ge(s_ev[4], j * (2 * CHUNK) + (unit + 1))
                            for k in range(KD):
                                last = mm(psum[2 + unit % 6][:, :], h1t_ring[:, v, k * P:(k + 1) * P],
                                          w_proj[:, k, side * 2 * DIM:(side + 1) * 2 * DIM], start=k == 0, stop=k == KD - 1)
                            last.then_inc(s_up[4], 1)
            pe.wait_ge(s_ev[4], 2 * TILES + BANKS[4])

            def flip(j, u):
                pe.wait_ge(s_hot[1], j * UNROLL + (u + 1))
                o = u % 4 * P
                nc.tensor.transpose(psum[4 + u % 2][:, 0:P], onehot[:, o:o + P], ident[:, :]).then_inc(s_flip, 1)

            flip(0, 0)
            with pe.Fori(0, ROUNDS) as j:
                for h in range(2):
                    tile = node_tiles(PE, j, h)
                    for u in range(h * GROUP, (h + 1) * GROUP):
                        flip(j, u + 1)
                        pe.wait_ge(s_flipped, j * UNROLL + (u + 1))
                        pe.wait_ge(s_used[0], j * UNROLL + (u + 1))
                        o = u % 4 * P
                        mm(psum[6 + u % 2][:, 0:DIM], onehot_t[:, o:o + P], region2[:, ds(tile[u - h * GROUP] * DIM, DIM)],
                           start=True, stop=True).then_inc(s_part[1], 1)

            pe.wait_ge(s_used[1], STEPS)
            for b, (h, c0, n) in enumerate(TURNS):
                for c in range(n):
                    last = nc.tensor.transpose(psum[b][:, c * P:(c + 1) * P], score3[:, (c0 + c) * P:(c0 + c + 1) * P, h], ident[:, :])
                last.then_inc(s_sm, 1)
            pe.wait_ge(s_sums, 1)
            for n, (o, w) in enumerate(((0, HC), (HC, HC), (2 * HC, STEP_CHUNKS), (2 * HC + STEP_CHUNKS, STEP_CHUNKS))):
                last = nc.tensor.transpose(psum[0][0:w, n * P:(n + 1) * P], row_sum[:, o:o + w], ident[:, :])
            last.then_inc(s_sumturn, 1)
            pe.wait_ge(s_rowdma, 192)
            for n in range(2):
                last = nc.tensor.transpose(psum[1][:, n * HC:(n + 1) * HC], sum_t[n], ident[0:HC, 0:HC])
            last.then_inc(s_sumturn, 1)
            for b, (h, c0, n) in enumerate(TURNS):
                pe.wait_ge(s_exp, h + 1)
                for c in range(n):
                    last = nc.tensor.transpose(psum[b][:, c * P:(c + 1) * P],
                                               score_rows[:, h * SC + (c0 + c) * P:h * SC + (c0 + c + 1) * P], ident[:, :])
                last.then_inc(s_sm, 1)

            pe.wait_ge(s_smev, len(TURNS))
            sum_pass(2)

            pe.wait_ge(s_added[2], STEPS + 4)
            transpose_stage(5, h_ring, s_hready)
            pe.wait_ge(s_wload, 16 * 8)

            def up(t, slot):
                pe.wait_ge(s_gelu, t + 1)
                for f in range(KF):
                    for k in range(KD):
                        last = mm(psum[2 * slot + f // 4][:, f % 4 * P:(f % 4 + 1) * P], w_up[:, k, f * P:(f + 1) * P],
                                  region1[:, ds(t * DIM + k * P, P)], start=k == 0, stop=k == KD - 1)
                last.then_inc(s_gup, 1)

            def down(t, slot):
                pe.wait_ge(s_gelu, t + 3)
                pe.wait_ge(s_ev[6], t + 1)
                for f in range(KF):
                    last = mm(psum[4 + slot][:, 0:DIM], gelu_t[:, slot, f, :], w_down[:, f, :], start=f == 0, stop=f == KF - 1)
                last.then_inc(s_up[6], 1)

            up(0, 0)
            with pe.Fori(0, TILES // 2) as i:
                up(i * 2 + 1, 1)
                down(i * 2, 0)
                up(i * 2 + 2, 0)
                down(i * 2 + 1, 1)
            down(TILES - 1, 0)

        @block.vector
        def _(dve):
            mine = Count(dve, s_dve)
            for n in (2, 4, 6):
                dve.sem_inc(s_ev[n], BANKS[n])
            dve.sem_inc(s_res1, CHUNK)
            dve.sem_inc(s_added[0], 4)
            dve.sem_inc(s_added[2], 4)
            dve.sem_inc(s_used[0], 2)
            dve.wait_ge(s_const, IOTAS)
            mine.did(dve.tensor_copy(iota_step, iota_i))
            mine.did(dve.tensor_copy(part_tile[:, :], part_i))
            mine.did(dve.memset(ones[:, :], 1.0))
            mine.settle()
            mine.did(dve.tensor_copy(iota_row[:, :], iota_step[:, 0:P]))
            mine.settle()
            mine.did(dve.tensor_scalar(ident[:, :], iota_row[:, :], part_tile[:, 0:1], None, ALU.is_equal))

            mine.did(dve.memset(ones_f, 1.0))
            dve.memset(dst_after, NO_NODE).then_inc(s_after, 1)
            dve.wait_ge(s_checkload, 48)
            mine.did(dve.tensor_tensor(descends, dst_here, dst_after, ALU.is_gt))
            mine.settle()
            dve.tensor_reduce(sort_cols[:, 0:1], descends, AX.X, ALU.add).then_inc(s_descents, 1)
            dve.wait_ge(s_check, 1)
            dve.tensor_scalar(unsorted, psum[0][0:1, 0:1], 1.0, None, ALU.min).then_inc(s_flag, 1)

            with if_unsorted(dve, DVE):
                sort = Count(dve, s_sort)
                before, total, base, base_one = (sort_cols[:, c:c + 1] for c in range(1, 5))
                sort.did(dve.tensor_scalar(earlier, iota_row[0:SR, 0:SR], part_tile[0:SR, 0:1], None, ALU.is_gt))
                sort.did(dve.memset(digit_mask, 1))
                dve.wait_ge(s_srcload, 16)
                sort.did(dve.tensor_copy(pairs[:, :, 0], dst_here))
                sort.did(dve.tensor_copy(pairs[:, :, 1], src_here))
                sort.settle()
                with dve.Fori(0, DST_BITS) as bit:
                    sort.enter(bit, 13)
                    sort.did(dve.tensor_tensor(place_i, pairs[:, :, 0], digit_mask.to_broadcast([SR, SORT_COLS]), ALU.bitwise_and))
                    sort.settle()
                    sort.did(dve.tensor_scalar(digit, place_i, 0.0, None, ALU.is_gt))
                    sort.did(dve.tensor_tensor(digit_mask, digit_mask, digit_mask, ALU.add))
                    sort.settle()
                    dve.tensor_tensor_scan(digits_before, digit, digit, 0.0, ALU.add, ALU.max).then_inc(s_digits, 1)
                    dve.wait_ge(s_prefix, bit + 1)
                    sort.did(dve.tensor_copy(before, psum[0][0:SR, 0:1]))
                    sort.did(dve.tensor_copy(total, psum[0][0:SR, 1:2]))
                    sort.settle()
                    sort.did(dve.scalar_tensor_tensor(base, part_tile[0:SR, 0:1], float(SORT_COLS), before, ALU.mult, ALU.subtract))
                    sort.did(dve.tensor_tensor(base_one, before, total, ALU.subtract))
                    sort.settle()
                    sort.did(dve.scalar_tensor_tensor(place, iota_step[0:SR, 0:SORT_COLS], base, digits_before, ALU.add, ALU.subtract))
                    sort.did(dve.tensor_scalar(place_one, digits_before, base_one, float(N_EDGES - 1), ALU.add, ALU.add))
                    sort.settle()
                    sort.did(dve.tensor_tensor(place_one, place_one, place, ALU.subtract))
                    sort.settle()
                    sort.did(dve.tensor_tensor(place_one, place_one, digit, ALU.mult))
                    sort.settle()
                    sort.did(dve.tensor_tensor(place, place, place_one, ALU.add))
                    sort.settle()
                    sort.did(dve.tensor_copy(place_i, place))
                    sort.settle()
                    dve.sem_inc(s_place, 1)
                    dve.wait_ge(s_pairs, bit * 16 + 16)
                sort.leave(DST_BITS)
                sort.did(dve.tensor_copy(dst_here, pairs[:, :, 0]))
                sort.did(dve.tensor_copy(src_here, pairs[:, :, 1]))
                sort.settle()
                dve.sem_inc(s_split, 1)

            def stats(region, j, u, width=DIM):
                dve.bn_stats(col(bn6, j, u, 6, 6), tile_of(region, j, u, width)).then_inc(s_stats, 1)

            def ln_factors(n):
                dve.wait_ge(s_stats, TILES * (n + 1))
                if n:
                    dve.wait_ge(s_norm, CHUNKS * n)
                half = bn6[:, :].rearrange("p (t s) -> p t s", s=6)
                mean_e, m2_e, mean_o, m2_o = (half[:, :, c] for c in (1, 2, 4, 5))
                mine.did(dve.tensor_tensor(mean2, mean_e, mean_o, ALU.add))
                mine.did(dve.tensor_tensor(diff, mean_e, mean_o, ALU.subtract))
                mine.did(dve.tensor_tensor(variance, m2_e, m2_o, ALU.add))
                mine.settle()
                mine.did(dve.tensor_tensor(diff2, diff, diff, ALU.mult))
                mine.settle()
                mine.did(dve.scalar_tensor_tensor(variance, diff2, DIM / 4.0, variance, ALU.mult, ALU.add))
                mine.settle()
                dve.tensor_scalar(variance, variance, 1.0 / DIM, EPS, ALU.mult, ALU.add).then_inc(s_var, 1)
                dve.wait_ge(s_std, n + 1)
                mine.did(dve.reciprocal(rstd[:, :], variance))
                mine.settle()
                dve.scalar_tensor_tensor(neg_mean[:, :], mean2, -0.5, rstd[:, :], ALU.mult, ALU.mult).then_inc(s_rstd, 1)

            with dve.Fori(0, CHUNKS) as j:
                dve.wait_ge(s_x, j * 16 + 32)
                for u in range(CHUNK):
                    stats(region0, j, u)
            ln_factors(0)

            dve.wait_ge(s_first, 16)
            mine.did(dve.tensor_scalar(first_t, first_i, 7, None, ALU.arith_shift_right))
            mine.settle()
            mine.did(dve.tensor_scalar(leave, first_t, float(TILES - 1), None, ALU.min))
            mine.settle()
            mine.did(dve.tensor_tensor(leave, leave, part_tile[:, :], ALU.add))
            mine.settle()
            for c in range(STEP_CHUNKS):
                dve.tensor_scalar(left[:, c * SC:(c + 1) * SC], iota_step, leave[:, c:c + 1], None, ALU.is_gt).then_inc(s_left, 1)
            dve.wait_ge(s_stair, 1)
            mine.did(dve.tensor_copy(edge_tile_f, psum[2][:, 0:STEP_CHUNKS]))
            mine.settle()
            dve.tensor_copy(edge_tile_i, edge_tile_f).then_inc(s_index, 1)
            for b in range(2):
                h0, h1 = b * (SC // 2), (b + 1) * (SC // 2)
                mine.did(dve.tensor_tensor(step_f[0:1, h0:h1], iota_step[0:1, h0:h1], psum[b][0:1, 0:SC // 2], ALU.subtract))
            mine.did(dve.tensor_tensor(node_tile_128, part_tile[:, :], edge_tile_f, ALU.subtract))
            mine.settle()
            mine.did(dve.tensor_scalar(step_f[0:1, :], step_f[0:1, :], float(TILES - 1), None, ALU.min))
            mine.did(dve.tensor_scalar(node_tile_128, node_tile_128, float(P), None, ALU.mult))
            mine.settle()
            dve.tensor_copy(node_tile[:, :], step_f[0:1, :]).then_inc(s_offsets, 1)
            dve.wait_ge(s_rowload, 16 * 4 * STEP_CHUNKS)
            for c in range(STEP_CHUNKS):
                mine.did(dve.tensor_scalar(dst_f[:, c * P:(c + 1) * P], row_dst[:, c * P:(c + 1) * P],
                                           node_tile_128[:, c:c + 1], None, ALU.subtract))
            mine.did(dve.tensor_copy(src_f, row_src))
            mine.settle()
            mine.did(dve.tensor_scalar(valid, dst_f, float(P), None, ALU.is_lt))
            mine.did(dve.tensor_scalar(differs, dst_f, 0.0, None, ALU.is_ge))
            mine.settle()
            dve.tensor_tensor(valid, valid, differs, ALU.mult).then_inc(s_tables, 1)
            dve.wait_ge(s_tables, 1)
            mine.did(dve.tensor_scalar(off_tile[:, :], valid, -1.0, BIG, ALU.add, ALU.mult))
            for other, out_brk in ((row_prev, break_fwd), (row_next, break_rev)):
                mine.did(dve.tensor_tensor(differs, row_dst, other, ALU.not_equal))
                mine.settle()
                mine.did(dve.scalar_tensor_tensor(out_brk[:, :], differs, -BIG, valid, ALU.mult, ALU.mult))
                mine.settle()
            dve.wait_ge(s_turned, 1)
            for b in range(2):
                n = min(4, STEP_CHUNKS - 4 * b) * P
                mine.did(dve.tensor_copy(src_step[:, b * 512:b * 512 + n], psum[3 + b][:, 0:n]))
                mine.did(dve.tensor_copy(dst_step[:, b * 512:b * 512 + n], psum[5 + b][:, 0:n]))
            mine.settle()
            dve.sem_inc(s_steps, 2)
            dve.wait_ge(s_offsets, 1)

            def make_onehot(n, j, u):
                o = u % 4 * P
                dve.tensor_scalar(onehot[:, o:o + P], iota_row[:, :], dst_step[:, ds(j * UNROLL + u, 1)], None,
                                  ALU.is_equal).then_inc(s_hot[n], 1)

            AHEAD = 3

            def add_partial(n, region, at, j, u):
                dve.wait_ge(s_part[n], j * UNROLL + (u + 1))
                dve.wait_ge(s_added[n], j * UNROLL + (u + 4))
                w = ACC_W if n == 2 else DIM
                acc = region[:, ds(at, w)]
                dve.tensor_tensor(acc, acc, psum[u % 4][:, 0:w], ALU.add).then_inc(s_added[n], 1)

            dve.wait_ge(s_zero1, 1)
            for u in range(AHEAD):
                make_onehot(0, 0, u)
            with dve.Fori(0, ROUNDS) as j:
                for h in range(2):
                    tile = node_tiles(DVE, j, h)
                    for u in range(h * GROUP, (h + 1) * GROUP):
                        make_onehot(0, j, u + AHEAD)
                        add_partial(0, region1, tile[u - h * GROUP] * ACC_W, j, u)

            dve.wait_ge(s_eps, 16)
            dve.wait_ge(s_bias, 16 * 9)
            dve.wait_ge(s_added[0], STEPS + 4)
            mine.did(dve.tensor_scalar(eps_gin[:, 1:2], eps_gin[:, 0:1], 1.0, None, ALU.add))
            mine.settle()
            with dve.Fori(0, CHUNKS) as j:
                for u in range(CHUNK):
                    dve.wait_ge(s_up[0], j * CHUNK + (u + 1))
                    dve.scalar_tensor_tensor(z_ring[:, u, :], tile_of(region0, j, u), eps_gin[:, 1:2],
                                             tile_of(region1, j, u, ACC_W), ALU.mult, ALU.add).then_inc(s_z, 1)

            dve.wait_ge(s_h0, 16 * CHUNKS)
            dve.wait_ge(s_z, TILES)
            with dve.Fori(0, CHUNKS) as j:
                mine.enter(j, 1)
                mine.did(dve.tensor_tensor(chunk(region0, j), chunk(region0, j), bias_over_chunk(0), ALU.add))
            mine.leave(CHUNKS)
            mine.settle()

            def evacuate_into_residual(n):
                with dve.Fori(0, CHUNKS) as j:
                    for u in range(CHUNK + 1):
                        if u < CHUNK:
                            dve.wait_ge(s_up[n], j * CHUNK + (CHUNK + u + 1))
                            dve.tensor_tensor(tile_of(region0, j, u), tile_of(region0, j, u), psum[4 + u % 4][:, 0:DIM],
                                              ALU.add).then_inc(s_ev[n], 1)
                        if u:
                            dve.wait_ge(s_ev[n], j * CHUNK + (BANKS[n] + u))
                            stats(region0, j, u - 1)

            evacuate_into_residual(2)
            ln_factors(1)
            dve.wait_ge(s_xr, 1 + 16 * (CHUNKS + 1))
            with dve.Fori(0, CHUNKS) as j:
                mine.enter(j, 2)
                dve.wait_ge(s_norm, j + (CHUNKS + 1))
                mine.did(dve.tensor_tensor(chunk(region0, j), chunk(region0, j), bias_over_chunk(1), ALU.mult))
                mine.settle()
                mine.did(dve.tensor_tensor(chunk(region0, j), chunk(region0, j), bias_over_chunk(2), ALU.add))
                mine.settle()
                dve.scalar_tensor_tensor(chunk(region2, j), chunk(region0, j), 0.0, chunk(region2, j), ALU.max,
                                         ALU.add).then_inc(s_x1, 1)
                dve.wait_ge(s_x1, j + 1)
                for u in range(CHUNK):
                    stats(region2, j, u)
            mine.leave(CHUNKS)
            ln_factors(2)
            dve.wait_ge(s_x1st, 16 * CHUNKS)
            def evacuate_projections(j, first):
                for u in range(CHUNK + 1):
                    if u < CHUNK:
                        dve.wait_ge(s_h1, j * CHUNK + (u + 1))
                        dve.tensor_tensor(tile_of(region0, j, u), h1_ring[:, u, :], bias(6), ALU.add).then_inc(s_res1, 1)
                    if u:
                        v = u - 1
                        a, b = psum[2 + 2 * v % 6], psum[2 + (2 * v + 1) % 6]
                        dve.wait_ge(s_up[4], j * (2 * CHUNK) + (2 * CHUNK + 2 * v + 1))
                        dve.tensor_tensor(tile_of(region2, j, v), a[:, 0:DIM], bias(3), ALU.add)
                        if not first:
                            dve.wait_ge(s_kv[v], j * 32)
                        dve.tensor_tensor(kv_stage[:, v, 0:DIM], a[:, DIM:2 * DIM], bias(4), ALU.add).then_inc(s_ev[4], 1)
                        dve.wait_ge(s_up[4], j * (2 * CHUNK) + (2 * CHUNK + 2 * v + 2))
                        dve.tensor_tensor(kv_stage[:, v, DIM:2 * DIM], b[:, 0:DIM], bias(5), ALU.add).then_inc(s_kvready, 1)
                        dve.wait_ge(s_res1, j * CHUNK + (CHUNK + v + 1))
                        dve.tensor_tensor(tile_of(region0, j, v), tile_of(region0, j, v), b[:, DIM:2 * DIM],
                                          ALU.add).then_inc(s_ev[4], 1)

            evacuate_projections(0, True)
            with dve.Fori(1, CHUNKS) as j:
                evacuate_projections(j, False)

            for b in range(CHUNK):
                dve.wait_ge(s_kv[b], 32 * CHUNKS)
            dve.wait_ge(s_ev[4], 2 * TILES + BANKS[4])
            for u in range(AHEAD):
                make_onehot(1, 0, u)
            with dve.Fori(0, ROUNDS) as j:
                for u in range(UNROLL + 1):
                    if u < UNROLL:
                        make_onehot(1, j, u + AHEAD)
                        dve.wait_ge(s_row[u], j * 16 + (16 * ROUNDS + 16))
                        dve.wait_ge(s_part[1], j * UNROLL + (u + 1))
                        dve.tensor_tensor(rows[:, u, :], rows[:, u, :], psum[6 + u % 2][:, 0:DIM], ALU.mult).then_inc(s_used[0], 1)
                    if u:
                        dve.wait_ge(s_used[0], j * UNROLL + (u + 2))
                        dve.tensor_reduce(score[:, ds(j * (UNROLL * HEADS) + (u - 1) * HEADS, HEADS)],
                                          rows[:, u - 1, :].rearrange("p (h d) -> p h d", h=HEADS), AX.X,
                                          ALU.add).then_inc(s_used[1], 1)

            lanes = lambda v: v.rearrange("p (c l) -> p c l", l=P)
            dve.wait_ge(s_flipped, STEPS)
            dve.wait_ge(s_flip, STEPS + 1)
            dve.wait_ge(s_part[1], STEPS)
            for inner, reset, brk, lane in ((inner_fwd, reset_fwd, break_fwd, 0), (inner_rev, reset_rev, break_rev, P - 1)):
                mine.did(dve.memset(inner, 1.0))
                mine.did(dve.tensor_copy(reset, brk[:, :]))
                mine.settle()
                mine.did(dve.memset(lanes(inner)[:, :, lane], 0.0))
                mine.did(dve.memset(lanes(reset)[:, :, lane], -BIG))
            mine.settle()
            mine.did(dve.tensor_tensor_scan(open_fwd, inner_fwd, break_fwd[:, :], 0.0, ALU.mult, ALU.min))
            mine.did(dve.tensor_tensor_scan(open_rev[:, ::-1], inner_rev[:, ::-1], break_rev[:, ::-1], 0.0, ALU.mult, ALU.min))
            for b, (h, c0, n) in enumerate(TURNS):
                dve.wait_ge(s_sm, b + 1)
                mine.did(dve.tensor_tensor(score_rows[:, h * SC + c0 * P:h * SC + (c0 + n) * P], psum[b][:, 0:n * P],
                                           off_tile[:, c0 * P:(c0 + n) * P], ALU.add))
            mine.settle()
            for h in range(HEADS):
                s, f, r = (v[:, h * SC:(h + 1) * SC] for v in (score_rows, fwd, rev))
                mine.did(dve.tensor_tensor_scan(f, reset_fwd, s, -BIG, ALU.add, ALU.max))
                mine.did(dve.tensor_tensor_scan(r[:, ::-1], reset_rev[:, ::-1], s[:, ::-1], -BIG, ALU.add, ALU.max))
            mine.settle()
            mine.did(dve.tensor_copy(row_sum[:, 0:HC], lanes(fwd)[:, :, P - 1]))
            mine.did(dve.tensor_copy(row_sum[:, HC:2 * HC], lanes(rev)[:, :, 0]))
            mine.did(dve.tensor_copy(row_sum[:, 2 * HC:2 * HC + STEP_CHUNKS], lanes(open_fwd)[:, :, P - 1]))
            mine.did(dve.tensor_copy(row_sum[:, 2 * HC + STEP_CHUNKS:2 * HC + 2 * STEP_CHUNKS], lanes(open_rev)[:, :, 0]))
            mine.settle()
            dve.sem_inc(s_sums, 1)
            dve.wait_ge(s_sumturn, 1)
            mine.did(dve.tensor_copy(rows_buf[0:HC, 0:2 * P], psum[0][0:HC, 0:2 * P]))
            mine.did(dve.tensor_copy(rows_buf[0:STEP_CHUNKS, 2 * P:4 * P], psum[0][0:STEP_CHUNKS, 2 * P:4 * P]))
            mine.settle()
            dve.sem_inc(s_rowsum, 1)
            dve.wait_ge(s_rowdma, 128)
            mine.did(dve.memset(line_out[0][:, 0:1], -BIG))
            mine.did(dve.memset(line_out[1][:, SC - 1:SC], -BIG))
            mine.did(dve.tensor_tensor_scan(line_out[0][:, 1:SC], line_brk[0][:, 0:SC - 1], line_val[0][:, 0:SC - 1], -BIG, ALU.add, ALU.max))
            mine.did(dve.tensor_tensor_scan(line_out[1][:, 0:SC - 1][:, ::-1], line_brk[1][:, 1:SC][:, ::-1],
                                            line_val[1][:, 1:SC][:, ::-1], -BIG, ALU.add, ALU.max))
            mine.settle()
            dve.sem_inc(s_carry, 1)
            dve.wait_ge(s_sumturn, 2)
            mine.did(dve.tensor_copy(row_sum[:, 0:2 * HC], psum[1][:, 0:2 * HC]))
            mine.settle()
            grid = lambda v: v.rearrange("p (h c l) -> p h c l", h=HEADS, l=P)
            for n, (opened, best) in enumerate(((open_fwd, fwd), (open_rev, rev))):
                carry_in = row_sum[:, n * HC:(n + 1) * HC].rearrange("p (h c) -> p h c", h=HEADS).unsqueeze(3).to_broadcast([P, HEADS, STEP_CHUNKS, P])
                still = lanes(opened).unsqueeze(1).to_broadcast([P, HEADS, STEP_CHUNKS, P])
                mine.did(dve.tensor_tensor(grid(carried), still, carry_in, ALU.add))
                mine.settle()
                mine.did(dve.tensor_tensor(best, best, carried, ALU.max))
                mine.settle()
            mine.did(dve.tensor_tensor(rev, rev, fwd, ALU.max))
            mine.settle()
            for h in range(HEADS):
                v = slice(h * SC, (h + 1) * SC)
                dve.tensor_tensor(fwd[:, v], score_rows[:, v], rev[:, v], ALU.subtract).then_inc(s_log, 1)
            for b, (h, c0, n) in enumerate(TURNS):
                dve.wait_ge(s_sm, len(TURNS) + b + 1)
                dve.tensor_copy(score3[:, c0 * P:(c0 + n) * P, h], psum[b][:, 0:n * P]).then_inc(s_smev, 1)
            dve.wait_ge(s_smev, len(TURNS))

            dve.wait_ge(s_zero2, 1)
            for u in range(AHEAD):
                make_onehot(2, 0, u)
            with dve.Fori(0, ROUNDS) as j:
                for h in range(2):
                    tile = node_tiles(DVE, j, h)
                    for u in range(h * GROUP, (h + 1) * GROUP):
                        make_onehot(2, j, u + AHEAD)
                        add_partial(2, region2, tile[u - h * GROUP] * ACC_W, j, u)

            dve.wait_ge(s_added[2], STEPS + 4)
            mine.did(dve.tensor_scalar(denom[:, :].rearrange("p (t h) -> p t h", h=HEADS), attn[:, :, DIM:ACC_W], 1e-16, None, ALU.add))
            mine.settle()
            mine.did(dve.reciprocal(denom[:, :], denom[:, :]))
            mine.settle()
            with dve.Fori(0, CHUNKS) as j:
                mine.enter(j, 1)
                sums = chunk(region2, j, ACC_W)
                by_head = sums.rearrange("p t (h d) -> p t h d", h=HEADS)
                w = denom[:, ds(j * (CHUNK * HEADS), CHUNK * HEADS)].rearrange("p (t h) -> p t h", h=HEADS)
                mine.did(dve.tensor_tensor(by_head, by_head, w.unsqueeze(3).to_broadcast([P, CHUNK, HEADS, HEAD_DIM]), ALU.mult))
                mine.settle()
                dve.tensor_tensor(chunk(region0, j), chunk(region0, j), sums, ALU.add).then_inc(s_res, 1)
                dve.wait_ge(s_res, j + 1)
                for u in range(CHUNK):
                    stats(region0, j, u)
            mine.leave(CHUNKS)
            ln_factors(3)
            dve.wait_ge(s_bias, 16 * 14)
            with dve.Fori(0, CHUNKS) as j:
                mine.enter(j, 2)
                dve.wait_ge(s_norm, j + (3 * CHUNKS + 1))
                mine.did(dve.tensor_tensor(chunk(region0, j), chunk(region0, j), bias_over_chunk(1), ALU.mult))
                mine.settle()
                for u in range(CHUNK):
                    dve.wait_ge(s_up[5], j * CHUNK + (u + 1))
                    dve.tensor_tensor(h_ring[:, u, :], tile_of(region0, j, u), bias(2), ALU.add).then_inc(s_hready, 1)
                dve.wait_ge(s_hready, j * CHUNK + CHUNK)
                mine.did(dve.tensor_tensor(chunk(region0, j), h_ring, bias_over_chunk(0), ALU.add))
            mine.leave(CHUNKS)
            mine.settle()
            dve.sem_inc(s_hkept, 1)

            def add_ffn(t, slot):
                dve.wait_ge(s_up[6], t + 3)
                y = region0[:, ds(t * DIM, DIM)]
                dve.tensor_tensor(y, y, psum[4 + slot][:, 0:DIM], ALU.add).then_inc(s_ev[6], 1)
                dve.wait_ge(s_ev[6], t + 3)
                dve.bn_stats(bn6[:, ds(t * 6, 6)], y).then_inc(s_stats, 1)
            with dve.Fori(0, TILES // 2) as i:
                add_ffn(i * 2, 0)
                add_ffn(i * 2 + 1, 1)
            add_ffn(TILES - 1, 0)
            ln_factors(4)
            dve.wait_ge(s_x1, 17 * CHUNKS)
            with dve.Fori(0, CHUNKS) as j:
                mine.enter(j, 2)
                dve.wait_ge(s_norm, j + (4 * CHUNKS + 1))
                c0 = chunk(region0, j)
                mine.did(dve.tensor_tensor(c0, c0, bias_over_chunk(3), ALU.mult))
                mine.settle()
                mine.did(dve.tensor_tensor(c0, c0, bias_over_chunk(4), ALU.add))
                mine.settle()
                dve.tensor_tensor(c0, c0, chunk(region2, j), ALU.add).then_inc(s_y, 1)
            mine.leave(CHUNKS)


_NAMES = ["x", "src", "dst", "L0_gnn_W1", "L0_gnn_b1", "L0_gnn_W2", "L0_gnn_b2", "L0_gnn_eps", "L0_gnn_gamma",
          "L0_gnn_beta", "L1_gnn_Wq", "L1_gnn_bq", "L1_gnn_Wk", "L1_gnn_bk", "L1_gnn_Wv", "L1_gnn_bv",
          "L1_gnn_Wskip", "L1_gnn_bskip", "L1_gnn_ln1_g", "L1_gnn_ln1_b", "L1_gnn_W1", "L1_gnn_b1", "L1_gnn_W2",
          "L1_gnn_b2", "L1_gnn_ln2_g", "L1_gnn_ln2_b"]


def kernel(**inputs):
    import numpy as np
    import concourse.bacc as bacc
    from concourse.bass_utils import run_bass_kernel_spmd

    nc = bacc.Bacc("TRN2", target_bir_lowering=False, num_devices=1)
    arrays, aps = {}, {}
    for name in _NAMES:
        a = np.ascontiguousarray(inputs[name])
        if a.ndim == 0:
            a = a.reshape(1)
        arrays["in_" + name] = a
        aps[name] = nc.dram_tensor("in_" + name, a.shape, mybir.dt.from_np(a.dtype), kind="ExternalInput").ap()
    out = nc.dram_tensor("out_0", (N_NODES, DIM), mybir.dt.float32, kind="ExternalOutput").ap()
    l0 = {n[7:]: aps[n] for n in _NAMES if n.startswith("L0_gnn_")}
    l1 = {n[7:]: aps[n] for n in _NAMES if n.startswith("L1_gnn_")}
    gnn_kernel(nc, aps["x"], aps["src"], aps["dst"], l0, l1, out)
    result = run_bass_kernel_spmd(nc, [arrays], core_ids=[0])
    return result.results[0]["out_0"]
```

```python
from contextlib import ExitStack

import concourse.bass as bass
from concourse import mybir

N_NODES = 6250
N_EDGES = 100000
DIM = 256
HEADS = 4
HEAD_DIM = DIM // HEADS
FF = 4 * DIM
P = 128
TILES = -(-N_NODES // P)
TAIL = N_NODES - (TILES - 1) * P
CHUNK = 7
CHUNKS = TILES // CHUNK
KD = DIM // P
KF = FF // P
EDGE_TILES = -(-N_EDGES // P)
UNROLL = 16
GROUP = UNROLL // 2
STEPS = -(-(EDGE_TILES + TILES - 1) // UNROLL) * UNROLL
ROUNDS = STEPS // UNROLL
STEP_CHUNKS = -(-(STEPS + UNROLL) // P)
STEP_COLS = STEP_CHUNKS * P
LIST_ROWS = STEP_COLS + 1
SORT_ROWS = 125
SORT_COLS = N_EDGES // SORT_ROWS
DST_BITS = (N_NODES - 1).bit_length()
NO_NODE = 8191
ACC_W = DIM + HEADS
WARM_UP = 40
BIG = 1.5e38
EPS = 1e-5

assert SORT_ROWS * SORT_COLS == N_EDGES and SORT_COLS % GROUP == 0
assert CHUNKS * CHUNK == TILES and STEPS + UNROLL <= STEP_COLS


class Count:

    def __init__(self, eng, sem):
        self.eng, self.sem, self.base, self.k, self.j, self.per = eng, sem, 0, 0, None, 0

    def did(self, instruction):
        instruction.then_inc(self.sem, 1)
        self.k += 1

    def value(self):
        return self.base + self.k if self.j is None else self.j * self.per + (self.base + self.k)

    def settle(self):
        self.eng.wait_ge(self.sem, self.value())

    def enter(self, j, per, start=0):
        self.base, self.k, self.j, self.per = self.base + self.k - start * per, 0, j, per

    def leave(self, end):
        assert self.k == self.per, (self.k, self.per)
        self.base, self.k, self.j = self.base + end * self.per, 0, None


def gnn_kernel(nc, x, src, dst, l0, l1, out):
    f32, i32, bf16 = mybir.dt.float32, mybir.dt.int32, mybir.dt.bfloat16
    ALU, ACT, AX = mybir.AluOpType, mybir.ActivationFunctionType, mybir.AxisListType
    ds = bass.ds
    PE, DVE = mybir.EngineType.PE, mybir.EngineType.DVE

    with ExitStack() as ctx:
        def sb(name, shape, dt=f32):
            return ctx.enter_context(nc.sbuf_tensor(name, shape, dt))

        def sem(name):
            return ctx.enter_context(nc.semaphore(name))

        def dram(name, shape, dt=f32):
            return nc.dram_tensor(name, shape, dt, kind="Internal").ap()

        sorted_src = dram("sorted_src", [N_EDGES, 1], i32)
        sorted_dst = dram("sorted_dst", [N_EDGES, 1], i32)
        list_src = dram("list_src", [LIST_ROWS, P], i32)
        list_dst = dram("list_dst", [LIST_ROWS, P], i32)
        list_prev = dram("list_prev", [LIST_ROWS, P], i32)
        list_next = dram("list_next", [LIST_ROWS, P], i32)
        h0_rows = dram("h0_rows", [TILES * P, DIM])
        k_rows = dram("k_rows", [TILES * P, DIM])
        v_rows = dram("v_rows", [TILES * P, DIM])
        x1_rows = dram("x1_rows", [TILES * P, DIM])
        turn_rows = dram("turn_rows", [4, HEADS * STEP_CHUNKS * P])

        edge_pairs = dram("edge_pairs", [N_EDGES, 2], i32)

        region0 = sb("region0", [P, TILES * DIM])
        region1 = sb("region1", [P, TILES * ACC_W])
        region2 = sb("region2", [P, TILES * ACC_W])
        rows_buf = sb("rows_buf", [P, UNROLL * DIM])
        score = sb("score", [P, STEP_COLS * HEADS])
        src_step = sb("src_step", [P, STEP_COLS], mybir.dt.int16)
        dst_step = sb("dst_step", [P, STEP_COLS])
        break_fwd = sb("break_fwd", [P, STEP_COLS], bf16)
        break_rev = sb("break_rev", [P, STEP_COLS], bf16)
        off_tile = sb("off_tile", [P, STEP_COLS], bf16)
        index_ring = sb("index_ring", [P, UNROLL], i32)
        onehots = sb("onehots", [P, 8 * P])
        onehot, onehot_t = onehots[:, 0:4 * P], onehots[:, 4 * P:8 * P]
        bias_rows = sb("bias_rows", [P, 7 * DIM])
        bias_cols = sb("bias_cols", [P, KF + KD])
        ident = sb("ident", [P, P])
        iota_row = sb("iota_row", [P, P])
        ones = sb("ones", [P, P], bf16)
        part_tile = sb("part_tile", [P, STEP_CHUNKS])
        bn6 = sb("bn6", [P, TILES * 6])
        rstd = sb("rstd", [P, TILES])
        neg_mean = sb("neg_mean", [P, TILES])
        eps_gin = sb("eps_gin", [P, 2])
        node_tile = sb("node_tile", [1, STEP_COLS], i32)
        row_sum = sb("row_sum", [P, (2 * HEADS + 2) * STEP_CHUNKS])
        ln_tmp = sb("ln_tmp", [P, 4 * TILES])
        mean2, diff, variance, diff2 = (ln_tmp[:, c * TILES:(c + 1) * TILES] for c in range(4))
        denom = ln_tmp

        psum = [ctx.enter_context(nc.psum_tensor(f"bank{b}", [P, 512], f32)) for b in range(8)]

        def tiles(region, width=DIM):
            return region[:, 0:TILES * width].rearrange("p (t w) -> p t w", w=width)

        attn = tiles(region2, ACC_W)

        def chunk(region, j, width=DIM, keep=DIM):
            v = region[:, ds(j * (CHUNK * width), CHUNK * width)]
            return v.rearrange("p (t w) -> p t w", w=width)[:, :, 0:keep]

        def tile_of(region, j, u, width=DIM, keep=DIM):
            return region[:, ds(j * (CHUNK * width) + u * width, keep)]

        def col(t, j, u, n=1, stride=1, off=0):
            return t[:, ds(j * (CHUNK * stride) + u * stride + off, n)]

        def bias(n):
            return bias_rows[:, n * DIM:(n + 1) * DIM]

        def bias_over_chunk(n):
            return bias(n).unsqueeze(1).to_broadcast([P, CHUNK, DIM])

        PAIRS = [min(2, CHUNK - t) * DIM for t in range(0, CHUNK, 2)]

        def ln_work(n):
            o = n % 2 * 4 * CHUNK
            return [row_sum[:, o + c * CHUNK:o + (c + 1) * CHUNK] for c in range(4)]

        at = [0]

        def work(n, dt=f32):
            size = n if dt != bf16 else n // 2
            v = region2[:, at[0]:at[0] + size]
            at[0] += size
            return v if dt == f32 else v.bitcast(dt)

        iota_i = work(STEP_COLS, i32)
        iota_step = work(STEP_COLS)
        part_i = work(STEP_CHUNKS, i32)
        first_i = work(STEP_CHUNKS, i32)
        first_t = work(STEP_CHUNKS, i32)
        leave = work(STEP_CHUNKS)
        edge_tile_f = work(STEP_CHUNKS)
        edge_tile_i = work(STEP_CHUNKS, i32)
        node_tile_128 = work(STEP_CHUNKS)
        left = work(STEP_CHUNKS * STEP_COLS, bf16)
        row_src = work(STEP_COLS, i32)
        row_dst = work(STEP_COLS, i32)
        row_prev = work(STEP_COLS, i32)
        row_next = work(STEP_COLS, i32)
        src_f = work(STEP_COLS)
        dst_f = work(STEP_COLS)
        valid = work(STEP_COLS)
        differs = work(STEP_COLS)
        step_f = differs
        pad_node = work(P, i32)
        pad_zero = work(P, i32)
        pad_first = work(1, i32)
        assert at[0] <= TILES * ACC_W

        SR = SORT_ROWS
        def sort_work(t, n, width=1, dt=f32):
            v = t[0:SR, n * SORT_COLS:(n + width) * SORT_COLS]
            return v if dt == f32 else v.bitcast(dt)
        dst_here = sort_work(score, 0, dt=i32)
        dst_after = sort_work(score, 1, dt=i32)
        descends = sort_work(score, 2)
        src_here = sort_work(score, 3, dt=i32)
        pairs = sort_work(rows_buf, 0, 2, i32).rearrange("p (c w) -> p c w", w=2)
        digit = sort_work(rows_buf, 2)
        digits_before = sort_work(rows_buf, 3)
        place_i = sort_work(rows_buf, 4, dt=i32)
        place = descends
        place_one = dst_after.bitcast(f32)
        earlier = onehot[0:SR, 0:SR]
        ones_f = onehot[0:SR, P:P + SR]
        sort_cols = onehot[0:SR, 2 * P:2 * P + 8]
        digit_mask = onehot[0:SR, 2 * P + 8:2 * P + 9].bitcast(i32)
        pair_stage = onehot[0:SR, 3 * P:3 * P + 2 * GROUP].bitcast(i32)
        place_stage = onehot[0:SR, 3 * P + 32:3 * P + 32 + GROUP].bitcast(i32)
        unsorted = onehot_t[0:1, 0:1].bitcast(i32)

        SC = STEP_COLS
        score_rows = region1[:, 0:HEADS * SC]
        fwd = region1[:, HEADS * SC:2 * HEADS * SC]
        rev = region1[:, 2 * HEADS * SC:3 * HEADS * SC]
        open_fwd = region1[:, 3 * HEADS * SC:3 * HEADS * SC + SC]
        open_rev = region1[:, 3 * HEADS * SC + SC:3 * HEADS * SC + 2 * SC]
        carried = score[:, 0:HEADS * SC]
        reset_fwd = bias_rows[:, 0:SC]
        reset_rev = bias_rows[:, SC:2 * SC]
        inner_fwd = onehot[:, 0:SC // 2].bitcast(bf16)
        inner_rev = onehot_t[:, 0:SC // 2].bitcast(bf16)
        HC = HEADS * STEP_CHUNKS
        sum_t = [rows_buf[0:HC, 0:P], rows_buf[0:HC, P:2 * P],
                 rows_buf[0:STEP_CHUNKS, 2 * P:3 * P], rows_buf[0:STEP_CHUNKS, 3 * P:4 * P]]
        line_val = [rows_buf[0:HEADS, 4 * P + n * SC:4 * P + (n + 1) * SC] for n in range(2)]
        line_brk = [rows_buf[0:HEADS, 4 * P + (2 + n) * SC:4 * P + (3 + n) * SC] for n in range(2)]
        line_out = [score[0:HEADS, n * SC:(n + 1) * SC] for n in range(2)]
        score3 = score[:, :].rearrange("p (s h) -> p s h", h=HEADS)
        TURNS = [(h, c, min(4, STEP_CHUNKS - c)) for h in range(HEADS) for c in range(0, STEP_CHUNKS, 4)]

        rows = rows_buf[:, :].rearrange("p (b w) -> p b w", w=DIM)
        w1_gin = rows_buf[:, 0:KD * DIM].rearrange("p (k n) -> p k n", k=KD)
        w2_gin = rows_buf[:, KD * DIM:2 * KD * DIM].rearrange("p (k n) -> p k n", k=KD)
        w_proj = rows_buf[:, 2 * KD * DIM:2 * KD * DIM + KD * 4 * DIM].rearrange("p (k n) -> p k n", k=KD)
        w_up = rows_buf[:, 0:KD * FF].rearrange("p (k n) -> p k n", k=KD)
        w_down = rows_buf[:, KD * FF:KD * FF + KF * DIM].rearrange("p (k n) -> p k n", k=KF)
        kv_stage = score[:, :].rearrange("p (t w) -> p t w", w=2 * DIM)
        z_ring = score[:, 0:CHUNK * DIM].rearrange("p (t w) -> p t w", w=DIM)
        h_ring = z_ring
        u_ring, h1_ring, h1t_ring = (region1[:, n * CHUNK * DIM:(n + 1) * CHUNK * DIM].rearrange("p (t w) -> p t w", w=DIM)
                                     for n in range(3))
        gelu_t = [score[:, CHUNK * DIM:CHUNK * DIM + FF].rearrange("p (f n) -> p f n", n=P),
                  onehots[:, 0:FF].rearrange("p (f n) -> p f n", n=P)]

        BANKS = {0: CHUNK, 1: 1, 2: 1, 3: 1, 4: 4, 5: 2, 6: 2}

        s_const = sem("const_ready")
        s_dve = sem("dve_done")
        s_x = sem("x_loaded")
        s_wload = sem("weights_loaded")
        s_lists = sem("edge_lists_copied")
        s_sorted = sem("sorted_edges_written")
        s_checkload = sem("check_lists_loaded")
        s_after = sem("padded_successors")
        s_descents = sem("descents_counted_by_row")
        s_check = sem("descents_summed")
        s_flag = sem("sorted_flag_ready")
        s_srcload = sem("sources_loaded")
        s_pairs = sem("pairs_loaded")
        s_digits = sem("digits_counted")
        s_prefix = sem("digit_prefix_ready")
        s_place = sem("places_ready")
        s_stage = sem("pairs_staged")
        s_scatter = [sem(f"pairs_scattered{c}") for c in range(GROUP)]
        s_split = sem("pairs_split")
        s_sort = sem("sort_steps")
        s_first = sem("first_destinations_loaded")
        s_left = sem("left_masks_ready")
        s_stair = sem("staircase_summed")
        s_index = sem("row_indices_ready")
        s_rowload = sem("edge_rows_gathered")
        s_tables = sem("row_tables_ready")
        s_turned = sem("tables_turned")
        s_steps = sem("step_tables_ready")
        s_offsets = sem("tile_offsets_ready")
        s_weighted = sem("values_weighted")
        s_hready = sem("ffn_input_ready")
        s_sums = sem("row_ends_ready")
        s_sumturn = sem("row_ends_turned")
        s_log = sem("exponents_ready")
        s_eps = sem("eps_loaded")
        s_bias = sem("biases_loaded")
        s_zero1 = sem("aggregate_zeroed")
        s_stats = [sem(f"layernorm_stats_ready{n}") for n in range(5)]
        s_var = [sem(f"layernorm_variance_ready{n}") for n in range(5)]
        s_std = [sem(f"layernorm_deviation_ready{n}") for n in range(5)]
        s_rstd = [sem(f"layernorm_rstd_ready{n}") for n in range(5)]
        s_norm = [sem(f"normalised{n}") for n in range(5)]
        s_h0 = sem("h0_stored")
        s_ring = sem("indices_copied")
        s_row = [sem(f"row_gathered{b}") for b in range(UNROLL)]
        s_used = [sem(f"row_used{n}") for n in range(3)]
        s_hot = [sem(f"onehot_ready{n}") for n in range(3)]
        s_part = [sem(f"partial_ready{n}") for n in range(3)]
        s_added = [sem(f"partial_added{n}") for n in range(3)]
        s_flip = sem("onehot_turned")
        s_flipped = sem("onehot_t_ready")
        s_z = sem("z_ready")
        s_h1 = sem("h1_ready")
        s_res1 = sem("h1_kept")
        s_up = [sem(f"stage_psum_ready{n}") for n in range(8)]
        s_ev = [sem(f"stage_evacuated{n}") for n in range(8)]
        s_xr = sem("x_reloaded")
        s_tail = sem("x_tail_zeroed")
        s_x1 = sem("x1_ready")
        s_x1st = sem("x1_stored")
        s_kv = [sem(f"kv_stored{b}") for b in range(CHUNK)]
        s_kvready = sem("kv_staged")
        s_sm = sem("softmax_turned")
        s_smev = sem("softmax_evacuated")
        s_rowsum = sem("row_summaries_ready")
        s_rowdma = sem("row_summaries_moved")
        s_carry = sem("carries_ready")
        s_zero2 = sem("sums_zeroed")
        s_exp = sem("weights_ready")
        s_gelu = sem("gelu_ready")
        s_gup = sem("hidden_psum_ready")
        s_res = sem("residual_ready")
        s_y = sem("output_ready")
        s_out = sem("output_stored")

        TAIL_ZERO, PADS, IOTAS = 1, 4, 6

        def dense_bodies(eng, body, around=lambda j, start: None, after=lambda: None):
            body(0, network=True)
            body(1, network=True, norms=True)
            with eng.Fori(2, CHUNKS) as j:
                around(j, 2)
                body(j, network=True, norms=True, project=True)
            after()
            body(CHUNKS, norms=True, project=True)
            body(CHUNKS + 1, project=True)

        block = ctx.enter_context(nc.Block())

        def node_tiles(engine_type, j, half):
            _, v = nc.values_load_multi_w_load_instructions(
                node_tile[0:1, ds(j * UNROLL + half * GROUP, GROUP)], engines=[engine_type], min_val=0,
                max_val=TILES - 1, skip_runtime_bounds_check_because="the table is clamped to the tile count")
            return v

        def if_unsorted(eng, engine_type):
            eng.wait_ge(s_flag, 1)
            _, v = nc.values_load_multi_w_load_instructions(
                unsorted, engines=[engine_type], min_val=0, max_val=1,
                skip_runtime_bounds_check_because="a comparison's result")
            return eng.If(v[0])

        @block.sync
        def _(sp):
            def load_x_chunk(region, s, j):
                sp.dma_start(chunk(region, j),
                             x[ds(j * (CHUNK * P), CHUNK * P), :].rearrange("(t p) f -> p t f", p=P)).then_inc(s, 16)

            def load_x_tail(region, s):
                sp.dma_start(region[0:TAIL, (TILES - 1) * DIM:TILES * DIM], x[(TILES - 1) * P:N_NODES, :]).then_inc(s, 16)

            def load_x_last(region, s):
                t0 = (CHUNKS - 1) * CHUNK
                full = region[:, t0 * DIM:(TILES - 1) * DIM].rearrange("p (t w) -> p t w", w=DIM)
                sp.dma_start(full, x[t0 * P:(TILES - 1) * P, :].rearrange("(t p) f -> p t f", p=P)).then_inc(s, 16)

            for b in range(CHUNK):
                sp.sem_inc(s_kv[b], 32)
            flat_rows = lambda t, a, n: t[a:a + n * SORT_COLS].rearrange("(p c) -> p c", c=SORT_COLS)
            sp.dma_start(dst_here, flat_rows(dst, 0, SR)).then_inc(s_checkload, 16)
            sp.wait_ge(s_after, 1)
            sp.dma_start(dst_after[0:SR - 1, :], flat_rows(dst, 1, SR - 1)).then_inc(s_checkload, 16)
            sp.dma_start(dst_after[SR - 1:SR, 0:SORT_COLS - 1],
                         dst[(SR - 1) * SORT_COLS + 1:N_EDGES].rearrange("(a b) -> a b", a=1)).then_inc(s_checkload, 16)

            sp.wait_ge(s_const, TAIL_ZERO)
            load_x_tail(region0, s_x)
            sp.wait_ge(s_x, 16)
            with sp.Fori(0, CHUNKS - 1) as j:
                load_x_chunk(region0, s_x, j)
                sp.wait_ge(s_x, j * 16 + 32)
                sp.nop(nofuse=True)
            load_x_last(region0, s_x)

            with sp.Fori(0, CHUNKS) as j:
                sp.wait_ge(s_norm[0], j + 1)
                sp.nop(nofuse=True)
                sp.dma_start(h0_rows[ds(j * (CHUNK * P), CHUNK * P), :].rearrange("(t p) f -> p t f", p=P),
                             chunk(region0, j)).then_inc(s_h0, 16)

            sp.wait_ge(s_part[0], STEPS)
            def w_view(w):
                return w.rearrange("(k p) n -> p k n", p=P)
            loads = [(w1_gin, w_view(l0["W1"])), (w2_gin, w_view(l0["W2"])),
                     (w_proj[:, :, 0:DIM], w_view(l1["Wq"])), (w_proj[:, :, DIM:2 * DIM], w_view(l1["Wk"])),
                     (w_proj[:, :, 2 * DIM:3 * DIM], w_view(l1["Wv"])),
                     (w_proj[:, :, 3 * DIM:4 * DIM], w_view(l1["Wskip"]))]
            for d, s in loads:
                sp.dma_start(d, s).then_inc(s_wload, 16)

            def moves(j, network=False, norms=False, project=False):
                if project:
                    c = j - 2
                    for u in range(CHUNK):
                        if u == 5 and norms:
                            store_x1(j - 1)
                        sp.wait_ge(s_kvready, c * CHUNK + (u + 1))
                        sp.nop(nofuse=True)
                        at_rows = ds(c * (CHUNK * P) + u * P, P)
                        sp.dma_start(k_rows[at_rows, :], kv_stage[:, u, 0:DIM]).then_inc(s_kv[u], 16)
                        sp.dma_start(v_rows[at_rows, :], kv_stage[:, u, DIM:2 * DIM]).then_inc(s_kv[u], 16)
                elif norms:
                    store_x1(j - 1)
                if network:
                    sp.wait_ge(s_up[1], j * CHUNK + CHUNK)
                    sp.nop(nofuse=True)
                    load_x_chunk(region2, s_xr, j)

            def store_x1(c):
                sp.wait_ge(s_x1, c + 1)
                sp.nop(nofuse=True)
                sp.dma_start(x1_rows[ds(c * (CHUNK * P), CHUNK * P), :].rearrange("(t p) f -> p t f", p=P),
                             chunk(region2, c)).then_inc(s_x1st, 16)

            moves(0, network=True)
            moves(1, network=True, norms=True)
            with sp.Fori(2, CHUNKS - 1) as j:
                moves(j, network=True, norms=True, project=True)
            moves(CHUNKS - 1, norms=True, project=True)
            sp.wait_ge(s_tail, 1)
            load_x_tail(region2, s_xr)
            load_x_last(region2, s_xr)
            moves(CHUNKS, norms=True, project=True)
            moves(CHUNKS + 1, project=True)

            sp.wait_ge(s_rowsum, 1)
            for n in range(2):
                sp.dma_start(turn_rows[n, :].rearrange("(r p) -> r p", p=P), sum_t[n]).then_inc(s_rowdma, 16)
                sp.dma_start(turn_rows[2 + n, 0:SC].rearrange("(r p) -> r p", p=P), sum_t[2 + n]).then_inc(s_rowdma, 16)
            sp.wait_ge(s_rowdma, 64)
            for n in range(2):
                sp.dma_start(line_val[n], turn_rows[n, :].rearrange("(h s) -> h s", h=HEADS)).then_inc(s_rowdma, 16)
                sp.dma_start(line_brk[n], turn_rows[2 + n, 0:SC].partition_broadcast(HEADS)).then_inc(s_rowdma, 16)
            sp.wait_ge(s_carry, 1)
            for n in range(2):
                sp.dma_start(turn_rows[n, :].rearrange("(h s) -> h s", h=HEADS), line_out[n]).then_inc(s_rowdma, 16)
            sp.wait_ge(s_rowdma, 160)
            for n in range(2):
                sp.dma_start(sum_t[n], turn_rows[n, :].rearrange("(r p) -> r p", p=P)).then_inc(s_rowdma, 16)

            sp.wait_ge(s_part[2], STEPS)
            sp.dma_start(w_up, l1["W1"].rearrange("(k p) n -> p k n", p=P)).then_inc(s_wload, 16)
            sp.dma_start(w_down, l1["W2"].rearrange("(k p) n -> p k n", p=P)).then_inc(s_wload, 16)
            sp.wait_ge(s_x1st, 16 * CHUNKS)
            with sp.Fori(0, CHUNKS) as j:
                sp.wait_ge(s_res, j + 1)
                sp.nop(nofuse=True)
                sp.dma_start(chunk(region2, j),
                             x1_rows[ds(j * (CHUNK * P), CHUNK * P), :].rearrange("(t p) f -> p t f", p=P)).then_inc(s_x1, 16)
                sp.wait_ge(s_x1, j * 16 + (CHUNKS + 16))
                sp.nop(nofuse=True)
            with sp.Fori(0, CHUNKS - 1) as j:
                sp.wait_ge(s_y, j + 1)
                sp.nop(nofuse=True)
                sp.dma_start(out[ds(j * (CHUNK * P), CHUNK * P), :].rearrange("(t p) f -> p t f", p=P),
                             chunk(region0, j)).then_inc(s_out, 16)
            t0 = (CHUNKS - 1) * CHUNK
            sp.wait_ge(s_y, CHUNKS)
            sp.dma_start(out[t0 * P:(TILES - 1) * P, :].rearrange("(t p) f -> p t f", p=P),
                         region0[:, t0 * DIM:(TILES - 1) * DIM].rearrange("p (t w) -> p t w", w=DIM)).then_inc(s_out, 16)
            sp.dma_start(out[(TILES - 1) * P:N_NODES, :],
                         region0[0:TAIL, (TILES - 1) * DIM:TILES * DIM]).then_inc(s_out, 16)
            sp.wait_ge(s_out, 16 * (CHUNKS + 1))


        @block.gpsimd
        def _(pool):
            tail_from = TAIL // 32 * 32
            def constant(instruction, n):
                instruction.then_inc(s_const, 1)
                pool.wait_ge(s_const, n)

            constant(pool.memset(region0[tail_from:P, (TILES - 1) * DIM:TILES * DIM], 0.0), TAIL_ZERO)
            constant(pool.memset(pad_node, NO_NODE), 2)
            constant(pool.memset(pad_zero, 0), 3)
            constant(pool.memset(pad_first, -1), PADS)
            constant(pool.iota(iota_i, [[1, STEP_COLS]], base=0, channel_multiplier=0), 5)
            constant(pool.iota(part_i, [[P, STEP_CHUNKS]], base=0, channel_multiplier=1), IOTAS)
            pool.memset(region1[:, 0:TILES * ACC_W], 0.0).then_inc(s_zero1, 1)
            pool.wait_ge(s_zero1, 1)

            with if_unsorted(pool, mybir.EngineType.Pool):
                pool.dma_start(src_here, src.rearrange("(p c) -> p c", c=SORT_COLS)).then_inc(s_srcload, 16)
                with pool.Fori(0, DST_BITS) as bit:
                    pool.wait_ge(s_place, bit + 1)
                    pool.nop(nofuse=True)
                    with pool.Fori(0, SORT_COLS // GROUP) as g:
                        n = bit * (SORT_COLS // GROUP) + g
                        pool.tensor_copy(pair_stage, rows_buf[0:SR, ds(g * (2 * GROUP), 2 * GROUP)].bitcast(i32)).then_inc(s_stage, 1)
                        pool.wait_ge(s_stage, n * 2 + 1)
                        pool.tensor_copy(place_stage, rows_buf[0:SR, ds(g * GROUP + 4 * SORT_COLS, GROUP)].bitcast(i32)).then_inc(s_stage, 1)
                        pool.wait_ge(s_stage, n * 2 + 2)
                        pool.nop(nofuse=True)
                        for c in range(GROUP):
                            pool.indirect_dma_start(edge_pairs, bass.IndirectOffsetOnAxis(ap=place_stage[:, c:c + 1], axis=0),
                                                    pair_stage[:, 2 * c:2 * c + 2], None).then_inc(s_scatter[c], 16)
                        for c in range(GROUP):
                            pool.wait_ge(s_scatter[c], n * 16 + 16)
                            pool.nop(nofuse=True)
                    pool.dma_start(rows_buf[0:SR, 0:2 * SORT_COLS].bitcast(i32),
                                   edge_pairs.rearrange("(p c) w -> p (c w)", p=SR)).then_inc(s_pairs, 16)
                pool.wait_ge(s_split, 1)
                pool.dma_start(sorted_dst.rearrange("(p c) o -> p (c o)", p=SR), dst_here).then_inc(s_sorted, 16)
                pool.dma_start(sorted_src.rearrange("(p c) o -> p (c o)", p=SR), src_here).then_inc(s_sorted, 16)
            with pool.Else():
                for to, fr in ((sorted_src, src), (sorted_dst, dst)):
                    pool.dma_start(to.rearrange("(a b) o -> a (b o)", a=16), fr.rearrange("(a b) -> a b", a=16)).then_inc(s_sorted, 16)

            pool.wait_ge(s_index, 1)
            pool.wait_ge(s_lists, 16 * 13)
            for c in range(STEP_CHUNKS):
                for table, rows_out in ((list_src, row_src), (list_dst, row_dst), (list_prev, row_prev), (list_next, row_next)):
                    pool.indirect_dma_start(rows_out[:, c * P:(c + 1) * P], None, table,
                                            bass.IndirectOffsetOnAxis(ap=edge_tile_i[:, c:c + 1], axis=0)).then_inc(s_rowload, 16)

            def gather(n, table, used):
                def group(j, half, first):
                    g0 = half * GROUP
                    if not first:
                        pool.wait_ge(used, j * UNROLL + (g0 + GROUP - UNROLL))
                    pool.tensor_copy(index_ring[:, g0:g0 + GROUP],
                                     src_step[:, ds(j * UNROLL + g0, GROUP)]).then_inc(s_ring, 1)
                    pool.wait_ge(s_ring, j * 2 + (2 * ROUNDS * n + half + 1))
                    pool.nop(nofuse=True)
                    for b in range(g0, g0 + GROUP):
                        pool.indirect_dma_start(rows[:, b, :], None, table,
                                                bass.IndirectOffsetOnAxis(ap=index_ring[:, b:b + 1], axis=0)).then_inc(s_row[b], 16)
                group(0, 0, True)
                group(0, 1, True)
                with pool.Fori(1, ROUNDS) as j:
                    group(j, 0, False)
                    group(j, 1, False)

            pool.wait_ge(s_steps, 2)
            pool.wait_ge(s_h0, 16 * CHUNKS)
            gather(0, h0_rows, s_part[0])

            pool.wait_ge(s_up[1], TILES)
            pool.memset(region2[tail_from:P, (TILES - 1) * DIM:TILES * DIM], 0.0).then_inc(s_tail, 1)

            for b in range(CHUNK):
                pool.wait_ge(s_kv[b], 32 * CHUNKS + 32)
            pool.wait_ge(s_up[4], 2 * TILES + 2 * CHUNK)
            gather(1, k_rows, s_used[1])

            pool.wait_ge(s_part[1], STEPS)
            pool.memset(region2[:, 0:TILES * ACC_W], 0.0).then_inc(s_zero2, 1)
            pool.wait_ge(s_sumturn, 2)
            pool.wait_ge(s_used[1], STEPS)
            gather(2, v_rows, s_part[2])

        @block.scalar
        def _(act):
            for n in (0, 1, 3, 5):
                act.sem_inc(s_ev[n], BANKS[n])
            act.sem_inc(s_gelu, 2)
            flat = lambda t: t.rearrange("a b -> (a b)")
            act.wait_ge(s_sorted, 32)
            act.wait_ge(s_const, PADS)
            spans = [(list_src, sorted_src, 0, 0, N_EDGES, pad_zero), (list_dst, sorted_dst, 0, 0, N_EDGES, pad_node),
                     (list_prev, sorted_dst, 1, 0, N_EDGES, pad_node), (list_next, sorted_dst, 0, 1, N_EDGES - 1, pad_node)]
            total = LIST_ROWS * P
            for t, s, to, fr, n, pad in spans:
                tf, sf = flat(t), flat(s)
                act.dma_start(tf[to:to + n], sf[fr:fr + n]).then_inc(s_lists, 16)
                end = to + n
                whole = (total - end) // P * P
                act.dma_start(tf[end:total - whole].rearrange("(a b) -> a b", a=1),
                              pad[0:1, 0:total - whole - end]).then_inc(s_lists, 16)
                act.dma_start(tf[total - whole:total].rearrange("(a b) -> a b", b=P), pad[0:whole // P, :]).then_inc(s_lists, 16)
            act.dma_start(flat(list_prev)[0:1].rearrange("(a b) -> a b", a=1), pad_first[0:1, :]).then_inc(s_lists, 16)
            act.wait_ge(s_lists, 16 * 13)
            act.dma_start(first_i, list_dst[1:STEP_COLS + 1, 0:1].rearrange("(c p) o -> p (c o)", p=P),
                          allow_slow_non_contiguous=True).then_inc(s_first, 16)
            act.dma_start(eps_gin[:, 0:1], l0["eps"].partition_broadcast(P)).then_inc(s_eps, 16)
            row = lambda v: v.partition_broadcast(P)
            for n, v in enumerate((l0["b2"], l0["gamma"], l0["beta"], l1["bq"], l1["bk"], l1["bv"], l1["bskip"])):
                act.dma_start(bias(n), row(v)).then_inc(s_bias, 16)
            act.dma_start(bias_cols[:, 0:KD], l0["b1"].rearrange("(c p) -> p c", p=P), allow_slow_non_contiguous=True).then_inc(s_bias, 16)
            act.dma_start(bias_cols[:, KD:KD + KF], l1["b1"].rearrange("(c p) -> p c", p=P), allow_slow_non_contiguous=True).then_inc(s_bias, 16)

            def norm_tile(dest, source, func, j, u):
                return act.activation(dest, tile_of(source, j, u), func, scale=col(rstd, j, u), bias=col(neg_mean, j, u))

            def norm_factors(n):
                act.wait_ge(s_var[n], 1)
                act.activation(variance, variance, ACT.Sqrt).then_inc(s_std[n], 1)
                act.wait_ge(s_rstd[n], 1)

            def deviation(n, c):
                act.wait_ge(s_var[n], c + 1)
                act.activation(ln_work(n)[2], ln_work(n)[2], ACT.Sqrt).then_inc(s_std[n], 1)

            def apply_norm(n, c):
                act.wait_ge(s_rstd[n], c + 1)
                for u in range(CHUNK):
                    last = norm_tile(tile_of(region0, c, u), region0, ACT.Identity, c, u)
                last.then_inc(s_norm[n], 1)

            def normalise(n, source, func):
                norm_factors(n)
                with act.Fori(0, CHUNKS) as j:
                    for u in range(CHUNK):
                        last = norm_tile(tile_of(region0, j, u), source, func, j, u)
                    last.then_inc(s_norm[n], 1)

            normalise(0, region0, ACT.Relu)

            def evacuate_transposed(n, dest):
                with act.Fori(0, CHUNKS) as j:
                    for u in range(CHUNK):
                        act.wait_ge(s_up[n], j * CHUNK + (CHUNK + u + 1))
                        act.activation(tile_of(dest, j, u), psum[u][:, 0:DIM], ACT.Copy).then_inc(s_ev[n], 1)

            act.wait_ge(s_bias, 16 * 9)
            evacuate_transposed(0, region2)

            def hidden(c, u):
                act.wait_ge(s_up[1], c * CHUNK + (u + 1))
                act.wait_ge(s_up[2], c * CHUNK + (u + 1))
                for k in range(KD):
                    last = act.activation(u_ring[:, u, k * P:(k + 1) * P], psum[0][:, k * P:(k + 1) * P],
                                          ACT.Relu, bias=bias_cols[:, k:k + 1])
                last.then_inc(s_ev[1], 1)

            def evacuate_h1_t(c, u):
                act.wait_ge(s_up[3], c * CHUNK + (CHUNK + u + 1))
                act.wait_ge(s_up[4], c * (2 * CHUNK) + (2 * u + 2))
                act.activation(h1t_ring[:, u, :], psum[2][:, 0:DIM], ACT.Copy).then_inc(s_ev[3], 1)

            def h1_chunk(c):
                act.wait_ge(s_rstd[2], c + 1)
                act.wait_ge(s_res1, c + 1)
                for u in range(CHUNK):
                    act.wait_ge(s_up[3], c * CHUNK + (u + 1))
                    norm_tile(h1_ring[:, u, :], region2, ACT.Relu, c, u).then_inc(s_h1, 1)

            def dense_act(j, network=False, norms=False, project=False):
                if project:
                    evacuate_h1_t(j - 2, 0)
                for u in range(CHUNK):
                    if network:
                        hidden(j, u)
                    if norms:
                        if u == 1:
                            deviation(1, j - 1)
                        if u == 2:
                            apply_norm(1, j - 1)
                        if u == 5:
                            deviation(2, j - 1)
                    if project and u < CHUNK - 1:
                        evacuate_h1_t(j - 2, u + 1)
                if norms:
                    h1_chunk(j - 1)
            dense_bodies(act, dense_act)

            with act.Fori(0, ROUNDS) as j:
                for u in range(UNROLL):
                    act.wait_ge(s_flip, j * UNROLL + (u + 1))
                    o = u % 4 * P
                    act.activation(onehot_t[:, o:o + P], psum[4 + u % 2][:, 0:P], ACT.Copy).then_inc(s_flipped, 1)

            act.wait_ge(s_carry, 1)
            for n, v in enumerate((l1["b2"], l1["ln1_g"], l1["ln1_b"], l1["ln2_g"], l1["ln2_b"])):
                act.dma_start(bias(n), row(v)).then_inc(s_bias, 16)
            for h in range(HEADS):
                act.wait_ge(s_log, h + 1)
                act.activation(score_rows[:, h * SC:(h + 1) * SC], fwd[:, h * SC:(h + 1) * SC], ACT.Exp,
                               scale=HEAD_DIM ** -0.5).then_inc(s_exp, 1)

            act.wait_ge(s_smev, len(TURNS))
            with act.Fori(0, ROUNDS) as j:
                for u in range(UNROLL):
                    act.wait_ge(s_row[u], j * 16 + (32 * ROUNDS + 16))
                    for h in range(HEADS):
                        part = rows[:, u, h * HEAD_DIM:(h + 1) * HEAD_DIM]
                        last = act.activation(part, part, ACT.Copy, scale=score[:, ds(j * (UNROLL * HEADS) + u * HEADS + h, 1)])
                    last.then_inc(s_weighted, 1)

            def evacuate_h_t(c):
                for p, w in enumerate(PAIRS):
                    act.wait_ge(s_up[5], c * len(PAIRS) + (len(PAIRS) + p + 1))
                    act.activation(region1[:, ds(c * (CHUNK * DIM) + 2 * p * DIM, w)], psum[6 + p % 2][:, 0:w],
                                   ACT.Copy).then_inc(s_ev[5], 1)

            def gelu(c, u):
                act.wait_ge(s_gup, c * CHUNK + (u + 1))
                act.wait_ge(s_up[6], c * CHUNK + (u + 1 + (u == 0)))
                for f in range(KF):
                    last = act.activation(gelu_t[u % 2][:, f, :], psum[2 * (u % 2) + f // 4][:, f % 4 * P:(f % 4 + 1) * P],
                                          ACT.Gelu, bias=bias_cols[:, KD + f:KD + f + 1])
                last.then_inc(s_gelu, 1)

            def ffn_chunk(j, first=False, last=False):
                for u in range(CHUNK):
                    gelu(j, u)
                    if u == 3:
                        if not first:
                            deviation(4, j - 1)
                        if not last:
                            deviation(3, j + 1)
                    if u == 4 and not last:
                        apply_norm(3, j + 1)
                    if u == 5 and not first:
                        apply_norm(4, j - 1)
                if not last:
                    evacuate_h_t(j + 1)

            deviation(3, 0)
            apply_norm(3, 0)
            evacuate_h_t(0)
            ffn_chunk(0, first=True)
            with act.Fori(1, CHUNKS - 1) as j:
                ffn_chunk(j)
            ffn_chunk(CHUNKS - 1, last=True)
            deviation(4, CHUNKS - 1)
            apply_norm(4, CHUNKS - 1)

        @block.tensor
        def _(pe):
            mm = nc.tensor.matmul
            for n in (0, 2, 3):
                pe.sem_inc(s_up[n], CHUNK)
            pe.sem_inc(s_up[5], len(PAIRS))
            pe.sem_inc(s_up[4], 2 * CHUNK)
            pe.sem_inc(s_up[6], 2)
            pe.wait_ge(s_descents, 1)
            mm(psum[0][0:1, 0:1], sort_cols[:, 0:1], ones_f[:, 0:1], start=True, stop=True).then_inc(s_check, 1)
            with if_unsorted(pe, PE):
                with pe.Fori(0, DST_BITS) as bit:
                    pe.wait_ge(s_digits, bit + 1)
                    ends = digits_before[:, SORT_COLS - 1:SORT_COLS]
                    mm(psum[0][0:SR, 0:1], earlier, ends, start=True, stop=True)
                    mm(psum[0][0:SR, 1:2], ones_f, ends, start=True, stop=True).then_inc(s_prefix, 1)
            pe.wait_ge(s_left, STEP_CHUNKS)
            left3 = left.rearrange("p (c s) -> p c s", c=STEP_CHUNKS)
            half = SC // 2
            for b in range(2):
                for c in range(STEP_CHUNKS):
                    last = mm(psum[b][0:1, 0:half], ones[:, 0:1], left3[:, c, b * half:(b + 1) * half],
                              start=c == 0, stop=c == STEP_CHUNKS - 1)
            for o in range(STEP_CHUNKS):
                for c in range(STEP_CHUNKS):
                    last = mm(psum[2][:, o:o + 1], left3[:, c, o * P:(o + 1) * P], ones[:, 0:1],
                              start=c == 0, stop=c == STEP_CHUNKS - 1)
            last.then_inc(s_stair, 1)
            pe.wait_ge(s_tables, 1)
            for n, t in enumerate((src_f, dst_f)):
                for c in range(STEP_CHUNKS):
                    last = nc.tensor.transpose(psum[3 + 2 * n + c // 4][:, c % 4 * P:(c % 4 + 1) * P], t[:, c * P:(c + 1) * P], ident[:, :])
            last.then_inc(s_turned, 1)

            def sum_pass(n):
                pe.wait_ge(s_steps, 2)
                if n == 0:
                    pe.wait_ge(s_row[0], 16)
                else:
                    pe.wait_ge(s_weighted, 1)
                for _ in range(WARM_UP):
                    mm(psum[7][:, 0:P], ident[:, :], ident[:, :], start=True, stop=True)
                with pe.Fori(0, ROUNDS) as j:
                    for u in range(UNROLL):
                        o = u % 4 * P
                        pe.wait_ge(s_hot[n], j * UNROLL + (u + 1))
                        if n == 0:
                            pe.wait_ge(s_row[u], j * 16 + 16)
                        else:
                            pe.wait_ge(s_weighted, j * UNROLL + (u + 1))
                        pe.wait_ge(s_added[n], j * UNROLL + (u + 1))
                        last = mm(psum[u % 4][:, 0:DIM], onehot[:, o:o + P], rows[:, u, :], start=True, stop=True)
                        if n == 2:
                            last = mm(psum[u % 4][:, DIM:ACC_W], onehot[:, o:o + P],
                                      score[:, ds(j * (UNROLL * HEADS) + u * HEADS, HEADS)], start=True, stop=True)
                        last.then_inc(s_part[n], 1)

            sum_pass(0)

            def transpose_tile(dest, place):
                for k in range(KD):
                    last = nc.tensor.transpose(dest[:, k * P:(k + 1) * P], place[:, k * P:(k + 1) * P], ident[:, :])
                return last

            def transpose_stage(n, ring, ready):
                with pe.Fori(0, CHUNKS) as j:
                    for u in range(CHUNK):
                        pe.wait_ge(ready, j * CHUNK + (u + 1))
                        pe.wait_ge(s_ev[n], j * CHUNK + (u + 1))
                        transpose_tile(psum[u], ring[:, u, :]).then_inc(s_up[n], 1)
                pe.wait_ge(s_ev[n], TILES + BANKS[n])

            pe.wait_ge(s_added[0], STEPS + 4)
            transpose_stage(0, z_ring, s_z)
            pe.wait_ge(s_wload, 16 * 6)

            def hidden(c, u):
                pe.wait_ge(s_ev[1], c * CHUNK + (u + 1))
                for f in range(KD):
                    for k in range(KD):
                        last = mm(psum[0][:, f * P:(f + 1) * P], w1_gin[:, k, f * P:(f + 1) * P],
                                  region2[:, ds(c * (CHUNK * DIM) + (u * DIM + k * P), P)], start=k == 0, stop=k == KD - 1)
                last.then_inc(s_up[1], 1)

            def layer_out(c, u):
                pe.wait_ge(s_ev[1], c * CHUNK + (u + 1 + BANKS[1]))
                pe.wait_ge(s_ev[2], c * CHUNK + (u + 1))
                for k in range(KD):
                    last = mm(psum[1][:, 0:DIM], u_ring[:, u, k * P:(k + 1) * P], w2_gin[:, k, :],
                              start=k == 0, stop=k == KD - 1)
                last.then_inc(s_up[2], 1)

            def turn_h1(c, u):
                pe.wait_ge(s_h1, c * CHUNK + (u + 1))
                pe.wait_ge(s_ev[3], c * CHUNK + (u + 1))
                transpose_tile(psum[2], h1_ring[:, u, :]).then_inc(s_up[3], 1)

            def project_half(c, u, side):
                pe.wait_ge(s_ev[3], c * CHUNK + (u + 1 + BANKS[3]))
                pe.wait_ge(s_ev[4], c * (2 * CHUNK) + (2 * u + side + 1 + 2 * (u == 0)))
                for k in range(KD):
                    last = mm(psum[4 + u % 2 * 2 + side][:, :], h1t_ring[:, u, k * P:(k + 1) * P],
                              w_proj[:, k, side * 2 * DIM:(side + 1) * 2 * DIM], start=k == 0, stop=k == KD - 1)
                last.then_inc(s_up[4], 1)

            def dense_pe(j, network=False, norms=False, project=False):
                if project:
                    turn_h1(j - 2, 0)
                for u in range(CHUNK):
                    if network:
                        hidden(j, u)
                    if project:
                        project_half(j - 2, u, 0)
                    if network:
                        layer_out(j, u)
                    if project:
                        if u < CHUNK - 1:
                            turn_h1(j - 2, u + 1)
                        project_half(j - 2, u, 1)
            dense_bodies(pe, dense_pe)
            pe.wait_ge(s_ev[4], 2 * TILES + BANKS[4])

            def flip(j, u):
                pe.wait_ge(s_hot[1], j * UNROLL + (u + 1))
                o = u % 4 * P
                nc.tensor.transpose(psum[4 + u % 2][:, 0:P], onehot[:, o:o + P], ident[:, :]).then_inc(s_flip, 1)

            flip(0, 0)
            with pe.Fori(0, ROUNDS) as j:
                for h in range(2):
                    tile = node_tiles(PE, j, h)
                    for u in range(h * GROUP, (h + 1) * GROUP):
                        flip(j, u + 1)
                        pe.wait_ge(s_flipped, j * UNROLL + (u + 1))
                        pe.wait_ge(s_used[0], j * UNROLL + (u + 1))
                        o = u % 4 * P
                        mm(psum[6 + u % 2][:, 0:DIM], onehot_t[:, o:o + P], region2[:, ds(tile[u - h * GROUP] * DIM, DIM)],
                           start=True, stop=True).then_inc(s_part[1], 1)

            pe.wait_ge(s_used[1], STEPS)
            for b, (h, c0, n) in enumerate(TURNS):
                for c in range(n):
                    last = nc.tensor.transpose(psum[b][:, c * P:(c + 1) * P], score3[:, (c0 + c) * P:(c0 + c + 1) * P, h], ident[:, :])
                last.then_inc(s_sm, 1)
            pe.wait_ge(s_sums, 1)
            for n, (o, w) in enumerate(((0, HC), (HC, HC), (2 * HC, STEP_CHUNKS), (2 * HC + STEP_CHUNKS, STEP_CHUNKS))):
                last = nc.tensor.transpose(psum[0][0:w, n * P:(n + 1) * P], row_sum[:, o:o + w], ident[:, :])
            last.then_inc(s_sumturn, 1)
            pe.wait_ge(s_rowdma, 192)
            for n in range(2):
                last = nc.tensor.transpose(psum[1][:, n * HC:(n + 1) * HC], sum_t[n], ident[0:HC, 0:HC])
            last.then_inc(s_sumturn, 1)
            for b, (h, c0, n) in enumerate(TURNS):
                pe.wait_ge(s_exp, h + 1)
                for c in range(n):
                    last = nc.tensor.transpose(psum[b][:, c * P:(c + 1) * P],
                                               score_rows[:, h * SC + (c0 + c) * P:h * SC + (c0 + c + 1) * P], ident[:, :])
                last.then_inc(s_sm, 1)

            pe.wait_ge(s_smev, len(TURNS))
            sum_pass(2)

            pe.wait_ge(s_added[2], STEPS + 4)

            def turn_h(c):
                pe.wait_ge(s_hready, c + 1)
                for p, w in enumerate(PAIRS):
                    pe.wait_ge(s_ev[5], c * len(PAIRS) + (p + 1))
                    for q in range(w // DIM):
                        last = transpose_tile(psum[6 + p % 2][:, q * DIM:(q + 1) * DIM], h_ring[:, 2 * p + q, :])
                    last.then_inc(s_up[5], 1)

            def up(c, u):
                pe.wait_ge(s_gelu, c * CHUNK + (u + 1 + (u == 0)))
                for f in range(KF):
                    for k in range(KD):
                        last = mm(psum[2 * (u % 2) + f // 4][:, f % 4 * P:(f % 4 + 1) * P], w_up[:, k, f * P:(f + 1) * P],
                                  region1[:, ds(c * (CHUNK * DIM) + (u * DIM + k * P), P)], start=k == 0, stop=k == KD - 1)
                last.then_inc(s_gup, 1)

            def down(c, u):
                pe.wait_ge(s_gelu, c * CHUNK + (u + 3))
                pe.wait_ge(s_ev[6], c * CHUNK + (u + 1 + (u == 0)))
                for f in range(KF):
                    last = mm(psum[4 + u % 2][:, 0:DIM], gelu_t[u % 2][:, f, :], w_down[:, f, :], start=f == 0, stop=f == KF - 1)
                last.then_inc(s_up[6], 1)

            def ffn_chunk(j, last=False):
                pe.wait_ge(s_ev[5], j * len(PAIRS) + (len(PAIRS) + BANKS[5]))
                for u in range(CHUNK):
                    up(j, u)
                    if u:
                        down(j, u - 1)
                if not last:
                    turn_h(j + 1)
                down(j, CHUNK - 1)

            turn_h(0)
            pe.wait_ge(s_wload, 16 * 8)
            with pe.Fori(0, CHUNKS - 1) as j:
                ffn_chunk(j)
            ffn_chunk(CHUNKS - 1, last=True)

        @block.vector
        def _(dve):
            mine = Count(dve, s_dve)
            for n in (2, 4, 6):
                dve.sem_inc(s_ev[n], BANKS[n])
            dve.sem_inc(s_res1, 1)
            dve.sem_inc(s_added[0], 4)
            dve.sem_inc(s_added[2], 4)
            dve.sem_inc(s_used[0], 2)
            dve.wait_ge(s_const, IOTAS)
            mine.did(dve.tensor_copy(iota_step, iota_i))
            mine.did(dve.tensor_copy(part_tile[:, :], part_i))
            mine.did(dve.memset(ones[:, :], 1.0))
            mine.settle()
            mine.did(dve.tensor_copy(iota_row[:, :], iota_step[:, 0:P]))
            mine.settle()
            mine.did(dve.tensor_scalar(ident[:, :], iota_row[:, :], part_tile[:, 0:1], None, ALU.is_equal))

            mine.did(dve.memset(ones_f, 1.0))
            dve.memset(dst_after, NO_NODE).then_inc(s_after, 1)
            dve.wait_ge(s_checkload, 48)
            mine.did(dve.tensor_tensor(descends, dst_here, dst_after, ALU.is_gt))
            mine.settle()
            dve.tensor_reduce(sort_cols[:, 0:1], descends, AX.X, ALU.add).then_inc(s_descents, 1)
            dve.wait_ge(s_check, 1)
            dve.tensor_scalar(unsorted, psum[0][0:1, 0:1], 1.0, None, ALU.min).then_inc(s_flag, 1)

            with if_unsorted(dve, DVE):
                sort = Count(dve, s_sort)
                before, total, base, base_one = (sort_cols[:, c:c + 1] for c in range(1, 5))
                sort.did(dve.tensor_scalar(earlier, iota_row[0:SR, 0:SR], part_tile[0:SR, 0:1], None, ALU.is_gt))
                sort.did(dve.memset(digit_mask, 1))
                dve.wait_ge(s_srcload, 16)
                sort.did(dve.tensor_copy(pairs[:, :, 0], dst_here))
                sort.did(dve.tensor_copy(pairs[:, :, 1], src_here))
                sort.settle()
                with dve.Fori(0, DST_BITS) as bit:
                    sort.enter(bit, 13)
                    sort.did(dve.tensor_tensor(place_i, pairs[:, :, 0], digit_mask.to_broadcast([SR, SORT_COLS]), ALU.bitwise_and))
                    sort.settle()
                    sort.did(dve.tensor_scalar(digit, place_i, 0.0, None, ALU.is_gt))
                    sort.did(dve.tensor_tensor(digit_mask, digit_mask, digit_mask, ALU.add))
                    sort.settle()
                    dve.tensor_tensor_scan(digits_before, digit, digit, 0.0, ALU.add, ALU.max).then_inc(s_digits, 1)
                    dve.wait_ge(s_prefix, bit + 1)
                    sort.did(dve.tensor_copy(before, psum[0][0:SR, 0:1]))
                    sort.did(dve.tensor_copy(total, psum[0][0:SR, 1:2]))
                    sort.settle()
                    sort.did(dve.scalar_tensor_tensor(base, part_tile[0:SR, 0:1], float(SORT_COLS), before, ALU.mult, ALU.subtract))
                    sort.did(dve.tensor_tensor(base_one, before, total, ALU.subtract))
                    sort.settle()
                    sort.did(dve.scalar_tensor_tensor(place, iota_step[0:SR, 0:SORT_COLS], base, digits_before, ALU.add, ALU.subtract))
                    sort.did(dve.tensor_scalar(place_one, digits_before, base_one, float(N_EDGES - 1), ALU.add, ALU.add))
                    sort.settle()
                    sort.did(dve.tensor_tensor(place_one, place_one, place, ALU.subtract))
                    sort.settle()
                    sort.did(dve.tensor_tensor(place_one, place_one, digit, ALU.mult))
                    sort.settle()
                    sort.did(dve.tensor_tensor(place, place, place_one, ALU.add))
                    sort.settle()
                    sort.did(dve.tensor_copy(place_i, place))
                    sort.settle()
                    dve.sem_inc(s_place, 1)
                    dve.wait_ge(s_pairs, bit * 16 + 16)
                sort.leave(DST_BITS)
                sort.did(dve.tensor_copy(dst_here, pairs[:, :, 0]))
                sort.did(dve.tensor_copy(src_here, pairs[:, :, 1]))
                sort.settle()
                dve.sem_inc(s_split, 1)

            def stats(n, region, j, u):
                dve.bn_stats(col(bn6, j, u, 6, 6), tile_of(region, j, u)).then_inc(s_stats[n], 1)

            def ln_factors():
                dve.wait_ge(s_stats[0], TILES)
                half = bn6[:, :].rearrange("p (t s) -> p t s", s=6)
                mean_e, m2_e, mean_o, m2_o = (half[:, :, c] for c in (1, 2, 4, 5))
                mine.did(dve.tensor_tensor(mean2, mean_e, mean_o, ALU.add))
                mine.did(dve.tensor_tensor(diff, mean_e, mean_o, ALU.subtract))
                mine.did(dve.tensor_tensor(variance, m2_e, m2_o, ALU.add))
                mine.settle()
                mine.did(dve.tensor_tensor(diff2, diff, diff, ALU.mult))
                mine.settle()
                mine.did(dve.scalar_tensor_tensor(variance, diff2, DIM / 4.0, variance, ALU.mult, ALU.add))
                mine.settle()
                dve.tensor_scalar(variance, variance, 1.0 / DIM, EPS, ALU.mult, ALU.add).then_inc(s_var[0], 1)
                dve.wait_ge(s_std[0], 1)
                mine.did(dve.reciprocal(rstd[:, :], variance))
                mine.settle()
                dve.scalar_tensor_tensor(neg_mean[:, :], mean2, -0.5, rstd[:, :], ALU.mult, ALU.mult).then_inc(s_rstd[0], 1)

            def ln_variance(n, c):
                mean2, diff, variance, diff2 = ln_work(n)
                dve.wait_ge(s_stats[n], c * CHUNK + CHUNK)
                half = bn6[:, ds(c * (6 * CHUNK), 6 * CHUNK)].rearrange("p (t s) -> p t s", s=6)
                mean_e, m2_e, mean_o, m2_o = (half[:, :, i] for i in (1, 2, 4, 5))
                mine.did(dve.tensor_tensor(mean2, mean_e, mean_o, ALU.add))
                mine.did(dve.tensor_tensor(diff, mean_e, mean_o, ALU.subtract))
                mine.did(dve.tensor_tensor(variance, m2_e, m2_o, ALU.add))
                mine.settle()
                mine.did(dve.tensor_tensor(diff2, diff, diff, ALU.mult))
                mine.settle()
                mine.did(dve.scalar_tensor_tensor(variance, diff2, DIM / 4.0, variance, ALU.mult, ALU.add))
                mine.settle()
                dve.tensor_scalar(variance, variance, 1.0 / DIM, EPS, ALU.mult, ALU.add).then_inc(s_var[n], 1)

            def ln_rstd(n, c):
                mean2, _, variance, _ = ln_work(n)
                r = rstd[:, ds(c * CHUNK, CHUNK)]
                dve.wait_ge(s_std[n], c + 1)
                dve.nop(nofuse=True)
                mine.did(dve.reciprocal(r, variance))
                mine.settle()
                dve.scalar_tensor_tensor(neg_mean[:, ds(c * CHUNK, CHUNK)], mean2, -0.5, r, ALU.mult,
                                         ALU.mult).then_inc(s_rstd[n], 1)

            with dve.Fori(0, CHUNKS) as j:
                dve.wait_ge(s_x, j * 16 + 32)
                for u in range(CHUNK):
                    stats(0, region0, j, u)
            ln_factors()

            dve.wait_ge(s_first, 16)
            mine.did(dve.tensor_scalar(first_t, first_i, 7, None, ALU.arith_shift_right))
            mine.settle()
            mine.did(dve.tensor_scalar(leave, first_t, float(TILES - 1), None, ALU.min))
            mine.settle()
            mine.did(dve.tensor_tensor(leave, leave, part_tile[:, :], ALU.add))
            mine.settle()
            for c in range(STEP_CHUNKS):
                dve.tensor_scalar(left[:, c * SC:(c + 1) * SC], iota_step, leave[:, c:c + 1], None, ALU.is_gt).then_inc(s_left, 1)
            dve.wait_ge(s_stair, 1)
            mine.did(dve.tensor_copy(edge_tile_f, psum[2][:, 0:STEP_CHUNKS]))
            mine.settle()
            dve.tensor_copy(edge_tile_i, edge_tile_f).then_inc(s_index, 1)
            for b in range(2):
                h0, h1 = b * (SC // 2), (b + 1) * (SC // 2)
                mine.did(dve.tensor_tensor(step_f[0:1, h0:h1], iota_step[0:1, h0:h1], psum[b][0:1, 0:SC // 2], ALU.subtract))
            mine.did(dve.tensor_tensor(node_tile_128, part_tile[:, :], edge_tile_f, ALU.subtract))
            mine.settle()
            mine.did(dve.tensor_scalar(step_f[0:1, :], step_f[0:1, :], float(TILES - 1), None, ALU.min))
            mine.did(dve.tensor_scalar(node_tile_128, node_tile_128, float(P), None, ALU.mult))
            mine.settle()
            dve.tensor_copy(node_tile[:, :], step_f[0:1, :]).then_inc(s_offsets, 1)
            dve.wait_ge(s_rowload, 16 * 4 * STEP_CHUNKS)
            for c in range(STEP_CHUNKS):
                mine.did(dve.tensor_scalar(dst_f[:, c * P:(c + 1) * P], row_dst[:, c * P:(c + 1) * P],
                                           node_tile_128[:, c:c + 1], None, ALU.subtract))
            mine.did(dve.tensor_copy(src_f, row_src))
            mine.settle()
            mine.did(dve.tensor_scalar(valid, dst_f, float(P), None, ALU.is_lt))
            mine.did(dve.tensor_scalar(differs, dst_f, 0.0, None, ALU.is_ge))
            mine.settle()
            dve.tensor_tensor(valid, valid, differs, ALU.mult).then_inc(s_tables, 1)
            dve.wait_ge(s_tables, 1)
            mine.did(dve.tensor_scalar(off_tile[:, :], valid, -1.0, BIG, ALU.add, ALU.mult))
            for other, out_brk in ((row_prev, break_fwd), (row_next, break_rev)):
                mine.did(dve.tensor_tensor(differs, row_dst, other, ALU.not_equal))
                mine.settle()
                mine.did(dve.scalar_tensor_tensor(out_brk[:, :], differs, -BIG, valid, ALU.mult, ALU.mult))
                mine.settle()
            dve.wait_ge(s_turned, 1)
            for b in range(2):
                n = min(4, STEP_CHUNKS - 4 * b) * P
                mine.did(dve.tensor_copy(src_step[:, b * 512:b * 512 + n], psum[3 + b][:, 0:n]))
                mine.did(dve.tensor_copy(dst_step[:, b * 512:b * 512 + n], psum[5 + b][:, 0:n]))
            mine.settle()
            dve.sem_inc(s_steps, 2)
            dve.wait_ge(s_offsets, 1)

            def make_onehot(n, j, u):
                o = u % 4 * P
                dve.tensor_scalar(onehot[:, o:o + P], iota_row[:, :], dst_step[:, ds(j * UNROLL + u, 1)], None,
                                  ALU.is_equal).then_inc(s_hot[n], 1)

            AHEAD = 3

            def add_partial(n, region, at, j, u):
                dve.wait_ge(s_part[n], j * UNROLL + (u + 1))
                dve.wait_ge(s_added[n], j * UNROLL + (u + 4))
                w = ACC_W if n == 2 else DIM
                acc = region[:, ds(at, w)]
                dve.tensor_tensor(acc, acc, psum[u % 4][:, 0:w], ALU.add).then_inc(s_added[n], 1)

            dve.wait_ge(s_zero1, 1)
            for u in range(AHEAD):
                make_onehot(0, 0, u)
            with dve.Fori(0, ROUNDS) as j:
                for h in range(2):
                    tile = node_tiles(DVE, j, h)
                    for u in range(h * GROUP, (h + 1) * GROUP):
                        make_onehot(0, j, u + AHEAD)
                        add_partial(0, region1, tile[u - h * GROUP] * ACC_W, j, u)

            dve.wait_ge(s_eps, 16)
            dve.wait_ge(s_bias, 16 * 9)
            dve.wait_ge(s_added[0], STEPS + 4)
            mine.did(dve.tensor_scalar(eps_gin[:, 1:2], eps_gin[:, 0:1], 1.0, None, ALU.add))
            mine.settle()
            with dve.Fori(0, CHUNKS) as j:
                for u in range(CHUNK):
                    dve.wait_ge(s_up[0], j * CHUNK + (u + 1))
                    dve.scalar_tensor_tensor(z_ring[:, u, :], tile_of(region0, j, u), eps_gin[:, 1:2],
                                             tile_of(region1, j, u, ACC_W), ALU.mult, ALU.add).then_inc(s_z, 1)

            dve.wait_ge(s_h0, 16 * CHUNKS)
            dve.wait_ge(s_z, TILES)

            def add_layer_out(c, u):
                dve.wait_ge(s_up[2], c * CHUNK + (CHUNK + u + 1))
                dve.tensor_tensor(tile_of(region0, c, u), tile_of(region0, c, u), psum[1][:, 0:DIM],
                                  ALU.add).then_inc(s_ev[2], 1)

            def take_half(c, u, side):
                bank = psum[4 + u % 2 * 2 + side]
                dve.wait_ge(s_up[4], c * (2 * CHUNK) + (2 * CHUNK + 2 * u + side + 1))
                if side == 0:
                    dve.tensor_tensor(tile_of(region2, c, u), bank[:, 0:DIM], bias(3), ALU.add)
                    dve.wait_ge(s_kv[u], c * 32 + 32)
                    dve.tensor_tensor(kv_stage[:, u, 0:DIM], bank[:, DIM:2 * DIM], bias(4), ALU.add).then_inc(s_ev[4], 1)
                else:
                    dve.tensor_tensor(kv_stage[:, u, DIM:2 * DIM], bank[:, 0:DIM], bias(5), ALU.add).then_inc(s_kvready, 1)
                    dve.tensor_tensor(tile_of(region0, c, u), tile_of(region0, c, u), bank[:, DIM:2 * DIM],
                                      ALU.add).then_inc(s_ev[4], 1)

            def dense_dve(j, network=False, norms=False, project=False):
                if network:
                    mine.did(dve.tensor_tensor(chunk(region0, j), chunk(region0, j), bias_over_chunk(0), ALU.add))
                if project:
                    dve.wait_ge(s_h1, (j - 2) * CHUNK + CHUNK)
                    dve.tensor_tensor(chunk(region0, j - 2), h1_ring, bias_over_chunk(6), ALU.add).then_inc(s_res1, 1)
                    dve.wait_ge(s_res1, (j - 2) + 2)
                    dve.wait_ge(s_x1st, (j - 2) * 16 + 16)
                if network:
                    mine.settle()
                for u in range(CHUNK):
                    if norms:
                        if u == 0:
                            ln_variance(1, j - 1)
                        if u == 2:
                            ln_rstd(1, j - 1)
                        if u == 3:
                            dve.wait_ge(s_norm[1], (j - 1) + 1)
                            mine.did(dve.tensor_tensor(chunk(region0, j - 1), chunk(region0, j - 1), bias_over_chunk(1), ALU.mult))
                            mine.settle()
                            mine.did(dve.tensor_tensor(chunk(region0, j - 1), chunk(region0, j - 1), bias_over_chunk(2), ALU.add))
                        if u == 4:
                            mine.settle()
                            dve.wait_ge(s_xr, j * 16 if network else 16 * (CHUNKS + 1))
                            dve.scalar_tensor_tensor(chunk(region2, j - 1), chunk(region0, j - 1), 0.0, chunk(region2, j - 1),
                                                     ALU.max, ALU.add).then_inc(s_x1, 1)
                            dve.wait_ge(s_x1, (j - 1) + 1)
                            for t in range(CHUNK):
                                stats(2, region2, j - 1, t)
                            ln_variance(2, j - 1)
                    if project:
                        take_half(j - 2, u, 0)
                    if network:
                        add_layer_out(j, u)
                    if norms and u == 5:
                        ln_rstd(2, j - 1)
                    if project:
                        take_half(j - 2, u, 1)
                    if network:
                        dve.wait_ge(s_ev[2], j * CHUNK + (BANKS[2] + u + 1))
                        stats(1, region0, j, u)
            dense_bodies(dve, dense_dve, lambda j, start: mine.enter(j, 15, start), lambda: mine.leave(CHUNKS))

            for b in range(CHUNK):
                dve.wait_ge(s_kv[b], 32 * CHUNKS + 32)
            dve.wait_ge(s_ev[4], 2 * TILES + BANKS[4])
            for u in range(AHEAD):
                make_onehot(1, 0, u)
            with dve.Fori(0, ROUNDS) as j:
                for u in range(UNROLL + 1):
                    if u < UNROLL:
                        make_onehot(1, j, u + AHEAD)
                        dve.wait_ge(s_row[u], j * 16 + (16 * ROUNDS + 16))
                        dve.wait_ge(s_part[1], j * UNROLL + (u + 1))
                        dve.tensor_tensor(rows[:, u, :], rows[:, u, :], psum[6 + u % 2][:, 0:DIM], ALU.mult).then_inc(s_used[0], 1)
                    if u:
                        dve.wait_ge(s_used[0], j * UNROLL + (u + 2))
                        dve.tensor_reduce(score[:, ds(j * (UNROLL * HEADS) + (u - 1) * HEADS, HEADS)],
                                          rows[:, u - 1, :].rearrange("p (h d) -> p h d", h=HEADS), AX.X,
                                          ALU.add).then_inc(s_used[1], 1)

            lanes = lambda v: v.rearrange("p (c l) -> p c l", l=P)
            dve.wait_ge(s_flipped, STEPS)
            dve.wait_ge(s_flip, STEPS + 1)
            dve.wait_ge(s_part[1], STEPS)
            for inner, reset, brk, lane in ((inner_fwd, reset_fwd, break_fwd, 0), (inner_rev, reset_rev, break_rev, P - 1)):
                mine.did(dve.memset(inner, 1.0))
                mine.did(dve.tensor_copy(reset, brk[:, :]))
                mine.settle()
                mine.did(dve.memset(lanes(inner)[:, :, lane], 0.0))
                mine.did(dve.memset(lanes(reset)[:, :, lane], -BIG))
            mine.settle()
            mine.did(dve.tensor_tensor_scan(open_fwd, inner_fwd, break_fwd[:, :], 0.0, ALU.mult, ALU.min))
            mine.did(dve.tensor_tensor_scan(open_rev[:, ::-1], inner_rev[:, ::-1], break_rev[:, ::-1], 0.0, ALU.mult, ALU.min))
            for b, (h, c0, n) in enumerate(TURNS):
                dve.wait_ge(s_sm, b + 1)
                mine.did(dve.tensor_tensor(score_rows[:, h * SC + c0 * P:h * SC + (c0 + n) * P], psum[b][:, 0:n * P],
                                           off_tile[:, c0 * P:(c0 + n) * P], ALU.add))
            mine.settle()
            for h in range(HEADS):
                s, f, r = (v[:, h * SC:(h + 1) * SC] for v in (score_rows, fwd, rev))
                mine.did(dve.tensor_tensor_scan(f, reset_fwd, s, -BIG, ALU.add, ALU.max))
                mine.did(dve.tensor_tensor_scan(r[:, ::-1], reset_rev[:, ::-1], s[:, ::-1], -BIG, ALU.add, ALU.max))
            mine.settle()
            mine.did(dve.tensor_copy(row_sum[:, 0:HC], lanes(fwd)[:, :, P - 1]))
            mine.did(dve.tensor_copy(row_sum[:, HC:2 * HC], lanes(rev)[:, :, 0]))
            mine.did(dve.tensor_copy(row_sum[:, 2 * HC:2 * HC + STEP_CHUNKS], lanes(open_fwd)[:, :, P - 1]))
            mine.did(dve.tensor_copy(row_sum[:, 2 * HC + STEP_CHUNKS:2 * HC + 2 * STEP_CHUNKS], lanes(open_rev)[:, :, 0]))
            mine.settle()
            dve.sem_inc(s_sums, 1)
            dve.wait_ge(s_sumturn, 1)
            mine.did(dve.tensor_copy(rows_buf[0:HC, 0:2 * P], psum[0][0:HC, 0:2 * P]))
            mine.did(dve.tensor_copy(rows_buf[0:STEP_CHUNKS, 2 * P:4 * P], psum[0][0:STEP_CHUNKS, 2 * P:4 * P]))
            mine.settle()
            dve.sem_inc(s_rowsum, 1)
            dve.wait_ge(s_rowdma, 128)
            mine.did(dve.memset(line_out[0][:, 0:1], -BIG))
            mine.did(dve.memset(line_out[1][:, SC - 1:SC], -BIG))
            mine.did(dve.tensor_tensor_scan(line_out[0][:, 1:SC], line_brk[0][:, 0:SC - 1], line_val[0][:, 0:SC - 1], -BIG, ALU.add, ALU.max))
            mine.did(dve.tensor_tensor_scan(line_out[1][:, 0:SC - 1][:, ::-1], line_brk[1][:, 1:SC][:, ::-1],
                                            line_val[1][:, 1:SC][:, ::-1], -BIG, ALU.add, ALU.max))
            mine.settle()
            dve.sem_inc(s_carry, 1)
            dve.wait_ge(s_sumturn, 2)
            mine.did(dve.tensor_copy(row_sum[:, 0:2 * HC], psum[1][:, 0:2 * HC]))
            mine.settle()
            grid = lambda v: v.rearrange("p (h c l) -> p h c l", h=HEADS, l=P)
            for n, (opened, best) in enumerate(((open_fwd, fwd), (open_rev, rev))):
                carry_in = row_sum[:, n * HC:(n + 1) * HC].rearrange("p (h c) -> p h c", h=HEADS).unsqueeze(3).to_broadcast([P, HEADS, STEP_CHUNKS, P])
                still = lanes(opened).unsqueeze(1).to_broadcast([P, HEADS, STEP_CHUNKS, P])
                mine.did(dve.tensor_tensor(grid(carried), still, carry_in, ALU.add))
                mine.settle()
                mine.did(dve.tensor_tensor(best, best, carried, ALU.max))
                mine.settle()
            mine.did(dve.tensor_tensor(rev, rev, fwd, ALU.max))
            mine.settle()
            for h in range(HEADS):
                v = slice(h * SC, (h + 1) * SC)
                dve.tensor_tensor(fwd[:, v], score_rows[:, v], rev[:, v], ALU.subtract).then_inc(s_log, 1)
            for b, (h, c0, n) in enumerate(TURNS):
                dve.wait_ge(s_sm, len(TURNS) + b + 1)
                dve.tensor_copy(score3[:, c0 * P:(c0 + n) * P, h], psum[b][:, 0:n * P]).then_inc(s_smev, 1)
            dve.wait_ge(s_smev, len(TURNS))

            dve.wait_ge(s_zero2, 1)
            for u in range(AHEAD):
                make_onehot(2, 0, u)
            with dve.Fori(0, ROUNDS) as j:
                for h in range(2):
                    tile = node_tiles(DVE, j, h)
                    for u in range(h * GROUP, (h + 1) * GROUP):
                        make_onehot(2, j, u + AHEAD)
                        add_partial(2, region2, tile[u - h * GROUP] * ACC_W, j, u)

            dve.wait_ge(s_added[2], STEPS + 4)
            mine.did(dve.tensor_scalar(denom[:, :].rearrange("p (t h) -> p t h", h=HEADS), attn[:, :, DIM:ACC_W], 1e-16, None, ALU.add))
            mine.settle()
            mine.did(dve.reciprocal(denom[:, :], denom[:, :]))
            mine.settle()
            dve.wait_ge(s_bias, 16 * 14)

            def take_sums(c):
                sums = chunk(region2, c, ACC_W)
                by_head = sums.rearrange("p t (h d) -> p t h d", h=HEADS)
                w = denom[:, ds(c * (CHUNK * HEADS), CHUNK * HEADS)].rearrange("p (t h) -> p t h", h=HEADS)
                mine.did(dve.tensor_tensor(by_head, by_head, w.unsqueeze(3).to_broadcast([P, CHUNK, HEADS, HEAD_DIM]), ALU.mult))
                mine.settle()
                dve.tensor_tensor(chunk(region0, c), chunk(region0, c), sums, ALU.add).then_inc(s_res, 1)

            def input_variance(c):
                dve.wait_ge(s_res, c + 1)
                for u in range(CHUNK):
                    stats(3, region0, c, u)
                ln_variance(3, c)

            def ffn_input(c):
                dve.wait_ge(s_norm[3], c + 1)
                mine.did(dve.tensor_tensor(chunk(region0, c), chunk(region0, c), bias_over_chunk(1), ALU.mult))
                mine.settle()
                dve.wait_ge(s_up[5], c * len(PAIRS) + len(PAIRS))
                dve.tensor_tensor(h_ring, chunk(region0, c), bias_over_chunk(2), ALU.add).then_inc(s_hready, 1)

            def keep_input(c):
                dve.wait_ge(s_hready, c + 1)
                mine.did(dve.tensor_tensor(chunk(region0, c), h_ring, bias_over_chunk(0), ALU.add))

            def add_ffn(c, u):
                y = tile_of(region0, c, u)
                dve.wait_ge(s_up[6], c * CHUNK + (u + 3))
                dve.tensor_tensor(y, y, psum[4 + u % 2][:, 0:DIM], ALU.add).then_inc(s_ev[6], 1)
                dve.wait_ge(s_ev[6], c * CHUNK + (u + 3))
                stats(4, region0, c, u)

            def gain(c):
                dve.wait_ge(s_norm[4], c + 1)
                mine.did(dve.tensor_tensor(chunk(region0, c), chunk(region0, c), bias_over_chunk(3), ALU.mult))

            def offset_and_x1(c):
                mine.settle()
                mine.did(dve.tensor_tensor(chunk(region0, c), chunk(region0, c), bias_over_chunk(4), ALU.add))
                mine.settle()
                dve.wait_ge(s_x1, c * 16 + (CHUNKS + 16))
                dve.tensor_tensor(chunk(region0, c), chunk(region0, c), chunk(region2, c), ALU.add).then_inc(s_y, 1)

            def ffn_chunk(j, first=False, last=False):
                mine.settle()
                for u in range(CHUNK):
                    add_ffn(j, u)
                    if u == 0:
                        if not last:
                            take_sums(j + 1)
                        if not first:
                            ln_variance(4, j - 1)
                    if u == 1 and not last:
                        input_variance(j + 1)
                    if u == 2:
                        if not first:
                            ln_rstd(4, j - 1)
                        if not last:
                            ln_rstd(3, j + 1)
                    if u == 4 and not last:
                        ffn_input(j + 1)
                    if u == 5:
                        if not last:
                            keep_input(j + 1)
                        if not first:
                            gain(j - 1)
                    if u == 6 and not first:
                        offset_and_x1(j - 1)

            take_sums(0)
            input_variance(0)
            ln_rstd(3, 0)
            ffn_input(0)
            keep_input(0)
            ffn_chunk(0, first=True)
            with dve.Fori(1, CHUNKS - 1) as j:
                mine.enter(j, 17, start=1)
                ffn_chunk(j)
            mine.leave(CHUNKS - 1)
            ffn_chunk(CHUNKS - 1, last=True)
            ln_variance(4, CHUNKS - 1)
            ln_rstd(4, CHUNKS - 1)
            gain(CHUNKS - 1)
            offset_and_x1(CHUNKS - 1)


_NAMES = ["x", "src", "dst", "L0_gnn_W1", "L0_gnn_b1", "L0_gnn_W2", "L0_gnn_b2", "L0_gnn_eps", "L0_gnn_gamma",
          "L0_gnn_beta", "L1_gnn_Wq", "L1_gnn_bq", "L1_gnn_Wk", "L1_gnn_bk", "L1_gnn_Wv", "L1_gnn_bv",
          "L1_gnn_Wskip", "L1_gnn_bskip", "L1_gnn_ln1_g", "L1_gnn_ln1_b", "L1_gnn_W1", "L1_gnn_b1", "L1_gnn_W2",
          "L1_gnn_b2", "L1_gnn_ln2_g", "L1_gnn_ln2_b"]


def kernel(**inputs):
    import numpy as np
    import concourse.bacc as bacc
    from concourse.bass_utils import run_bass_kernel_spmd

    nc = bacc.Bacc("TRN2", target_bir_lowering=False, num_devices=1)
    arrays, aps = {}, {}
    for name in _NAMES:
        a = np.ascontiguousarray(inputs[name])
        if a.ndim == 0:
            a = a.reshape(1)
        arrays["in_" + name] = a
        aps[name] = nc.dram_tensor("in_" + name, a.shape, mybir.dt.from_np(a.dtype), kind="ExternalInput").ap()
    out = nc.dram_tensor("out_0", (N_NODES, DIM), mybir.dt.float32, kind="ExternalOutput").ap()
    l0 = {n[7:]: aps[n] for n in _NAMES if n.startswith("L0_gnn_")}
    l1 = {n[7:]: aps[n] for n in _NAMES if n.startswith("L1_gnn_")}
    gnn_kernel(nc, aps["x"], aps["src"], aps["dst"], l0, l1, out)
    result = run_bass_kernel_spmd(nc, [arrays], core_ids=[0])
    return result.results[0]["out_0"]
```
